# Optimizing a Trainium2 kernel written in Bass

```python
import numpy as np
import jax
import jax.numpy as jnp

def _softmax(x, axis=-1):
    return jax.nn.softmax(x, axis=axis)

def _gelu(x):
    return jax.nn.gelu(x, approximate=True)

def _silu(x):
    return jax.nn.silu(x)

def _sigmoid(x):
    return jax.nn.sigmoid(x)

def _layernorm(x, axis=-1, eps=1e-05):
    m = jnp.mean(x, axis=axis, keepdims=True)
    v = jnp.var(x, axis=axis, keepdims=True)
    return (x - m) / jnp.sqrt(v + eps)

def _scatter_add(tgt, idx, src, axis=0):
    return tgt.at[idx].add(src)

def _segment_sum(src, seg, n):
    return jax.ops.segment_sum(src, seg, n)
kernel_name = 'mk_adj_ffn_d1_adj_r2_78831d'

def setup_inputs(seed: int=0):
    np.random.seed(seed)
    _w = jnp.asarray

    def _rec_inputs():
        import jax
        import jax.numpy as jnp
        _gk = jax.random.key(seed)
        x = -0.0002928 + 1 * jax.random.normal(jax.random.fold_in(_gk, 1), (32, 256, 128), jnp.float32)
        _a = jax.random.bernoulli(jax.random.fold_in(_gk, 2), 0.03125, (32, 256, 256))
        _a = jnp.logical_or(_a, jnp.swapaxes(_a, -1, -2))
        _a = jnp.logical_or(_a, jnp.eye(256, dtype=bool))
        _af = _a.astype(jnp.float32)
        _af = _af * jax.random.uniform(jax.random.fold_in(_gk, 3), (32, 256, 256), jnp.float32, 0.05, 1)
        adj = _af
        return (x, adj)
    x, adj = _rec_inputs()

    def _L0_gnn_setup():
        import jax, jax.numpy as jnp
        import numpy as np
        B, N, D, H = (8, 1024, 128, 512)
        RMS_EPS = 1e-06

        def _rmsnorm(h, w, eps=RMS_EPS):
            var = jnp.mean(jnp.square(h), axis=-1, keepdims=True)
            return h * jax.lax.rsqrt(var + eps) * w
        key = jax.random.key(seed)
        ks = jax.random.split(key, 5)
        x = jax.random.normal(ks[0], (B, N, D), dtype=jnp.float32)
        adjacency = jax.random.uniform(ks[1], (B, N, N), dtype=jnp.float32)
        epsilon = jnp.zeros((), dtype=jnp.float32)
        W1 = jax.random.normal(ks[2], (D, H), dtype=jnp.float32) * (1.0 / np.sqrt(D))
        b1 = jnp.zeros((H,), dtype=jnp.float32)
        rms_weight = jnp.ones((H,), dtype=jnp.float32)
        W2 = jax.random.normal(ks[3], (H, D), dtype=jnp.float32) * (1.0 / np.sqrt(H))
        b2 = jnp.zeros((D,), dtype=jnp.float32)
        return {'x': x, 'adjacency': adjacency, 'epsilon': epsilon, 'W1': W1, 'b1': b1, 'rms_weight': rms_weight, 'W2': W2, 'b2': b2}
    _L0_gnn_all = _L0_gnn_setup()
    _L0_gnn_in = {k: v for k, v in _L0_gnn_all.items() if k in ('epsilon', 'W1', 'b1', 'rms_weight', 'W2', 'b2')}
    del _L0_gnn_all

    def _L0_ffn_setup():
        import jax, jax.numpy as jnp
        import numpy as np
        N_EXPERTS = 8
        TOP_K = 2
        key = jax.random.key(seed)
        ks = jax.random.split(key, 5)
        B, T, C, E, H = (8, 1024, 128, 8, 341)
        scale = 1.0 / np.sqrt(C)
        return {'x': jax.random.normal(ks[0], (B, T, C), dtype=jnp.float32), 'router_w': jax.random.normal(ks[1], (E, C), dtype=jnp.float32) * scale, 'w1': jax.random.normal(ks[2], (E, H, C), dtype=jnp.float32) * scale, 'w2': jax.random.normal(ks[3], (E, C, H), dtype=jnp.float32) * (1.0 / np.sqrt(H)), 'w3': jax.random.normal(ks[4], (E, H, C), dtype=jnp.float32) * scale}
    _L0_ffn_all = _L0_ffn_setup()
    _L0_ffn_in = {k: v for k, v in _L0_ffn_all.items() if k in ('router_w', 'w1', 'w2', 'w3')}
    del _L0_ffn_all
    return {'x': x, 'adj': adj, 'L0_gnn_epsilon': _L0_gnn_in['epsilon'], 'L0_gnn_W1': _L0_gnn_in['W1'], 'L0_gnn_b1': _L0_gnn_in['b1'], 'L0_gnn_rms_weight': _L0_gnn_in['rms_weight'], 'L0_gnn_W2': _L0_gnn_in['W2'], 'L0_gnn_b2': _L0_gnn_in['b2'], 'L0_ffn_router_w': _L0_ffn_in['router_w'], 'L0_ffn_w1': _L0_ffn_in['w1'], 'L0_ffn_w2': _L0_ffn_in['w2'], 'L0_ffn_w3': _L0_ffn_in['w3']}

def reference(x, adj, L0_gnn_epsilon, L0_gnn_W1, L0_gnn_b1, L0_gnn_rms_weight, L0_gnn_W2, L0_gnn_b2, L0_ffn_router_w, L0_ffn_w1, L0_ffn_w2, L0_ffn_w3):
    import jax
    import jax.numpy as jnp

    def _L0_gnn_ref(x, adjacency, epsilon, W1, b1, rms_weight, W2, b2):
        import jax, jax.numpy as jnp
        import numpy as np
        B, N, D, H = (8, 1024, 128, 512)
        RMS_EPS = 1e-06

        def _rmsnorm(h, w, eps=RMS_EPS):
            var = jnp.mean(jnp.square(h), axis=-1, keepdims=True)
            return h * jax.lax.rsqrt(var + eps) * w
        neighbor_sum = jnp.einsum('bnm,bmd->bnd', adjacency, x)
        agg = epsilon * x + neighbor_sum
        h = jnp.einsum('bnd,dh->bnh', agg, W1) + b1
        h = jax.nn.silu(_rmsnorm(h, rms_weight))
        out = jnp.einsum('bnh,hd->bnd', h, W2) + b2
        return out

    def _L0_ffn_ref(x, router_w, w1, w2, w3):
        import jax, jax.numpy as jnp
        import numpy as np
        N_EXPERTS = 8
        TOP_K = 2
        B, T, C = x.shape
        flat = x.reshape(-1, C)
        logits = flat @ router_w.T
        probs = jax.nn.softmax(logits, axis=-1)
        topk_probs, topk_idx = jax.lax.top_k(probs, TOP_K)
        topk_probs = topk_probs / (jnp.sum(topk_probs, axis=-1, keepdims=True) + 1e-09)
        onehot = jax.nn.one_hot(topk_idx, N_EXPERTS, dtype=flat.dtype)
        gates = jnp.einsum('nk,nke->ne', topk_probs, onehot)
        h1 = jnp.einsum('nc,ehc->neh', flat, w1)
        h3 = jnp.einsum('nc,ehc->neh', flat, w3)
        h = jax.nn.silu(h1) * h3
        y = jnp.einsum('neh,ech->nec', h, w2)
        out = jnp.einsum('ne,nec->nc', gates, y)
        return out.reshape(B, T, C)
    x = x + _L0_gnn_ref(_layernorm(x, axis=-1), adj, L0_gnn_epsilon, L0_gnn_W1, L0_gnn_b1, L0_gnn_rms_weight, L0_gnn_W2, L0_gnn_b2)
    x = x + _L0_ffn_ref(_layernorm(x, axis=-1), L0_ffn_router_w, L0_ffn_w1, L0_ffn_w2, L0_ffn_w3)
    return x

_drawn_inputs = setup_inputs


def setup_inputs(seed=0):
    import zlib

    import numpy as np

    out = dict(_drawn_inputs(seed))
    spreads = {'L0_gnn_b1': (0.0, 0.1), 'L0_gnn_rms_weight': (1.0, 0.2), 'L0_gnn_b2': (0.0, 0.1)}
    factors = {}
    for name, (base, spread) in spreads.items():
        noise = np.random.default_rng([zlib.crc32(name.encode()), seed]).standard_normal(out[name].shape)
        drawn = base * np.exp(spread * noise) if base else spread * noise
        out[name] = jnp.asarray(drawn.astype(out[name].dtype))
    for name, factor in factors.items():
        out[name] = (out[name] * factor).astype(out[name].dtype)
    return out
```

```python
from contextlib import ExitStack

import concourse.bass as bass
from concourse import mybir

F32 = mybir.dt.float32
F32R = mybir.dt.float32r
BF16 = mybir.dt.bfloat16
I32 = mybir.dt.int32
U32 = mybir.dt.uint32
ALU = mybir.AluOpType
ACT = mybir.ActivationFunctionType
AX = mybir.AxisListType

P = 128
D = 128
N = 256
GRAPHS = 32
TOKENS = GRAPHS * N
TT = N // P
TILES = TOKENS // P
H = 512
HC = H // P
E = 8
EH = 341
EHP = EH + 1
CHUNKS = 3
HK = EHP // CHUNKS
TOP = 2
ROW = D + 2
CAP = TOKENS + P
SLOT_TILES = TOKENS * TOP // P + E
LN_EPS, RMS_EPS, GATE_EPS = 1e-5, 1e-6, 1e-9
UNROLL = 4


class Step:

    def __init__(self, k, off):
        self.k, self.off = k, off

    @property
    def n(self):
        return self.k * UNROLL + self.off if not isinstance(self.k, int) else self.k * UNROLL + self.off

    def ring(self, r):
        return self.off % r

    def turn(self, r):
        return self.k * (UNROLL // r) + self.off // r

    def plus(self, d):
        return Step(self.k, self.off + d)

    def within(self, count):
        return not isinstance(self.k, int) or 0 <= self.k * UNROLL + self.off < count


def positive(value):
    return not isinstance(value, int) or value > 0


def run_steps(eng, first, steady, bodies, last, step):
    for j in range(first, steady):
        step(Step(0, j))
    with eng.Fori(0, bodies) as k:
        for q in range(UNROLL):
            step(Step(k, steady + q))
    for j in range(steady + UNROLL * bodies, last + 1):
        step(Step(0, j))


def graph_moe_kernel(nc, x, adj_t, eps, w1, b1, rms_w, w2, b2, router_t, ew1, ew3, ew2, out):
    ctx = ExitStack()
    with ctx:
        def sb(name, shape, dt=F32):
            return ctx.enter_context(nc.sbuf_tensor(name, shape, dt))

        def bank(name, shape, dt=F32):
            return ctx.enter_context(nc.psum_tensor(name, shape, dt))

        def sem(name):
            return ctx.enter_context(nc.semaphore(name))

        expert_rows = nc.dram_tensor("expert_rows", (E * CAP + E * P, ROW), F32, kind="Internal").ap()
        results = nc.dram_tensor("results", (TOP * TOKENS + 2 * E * P, D), F32, kind="Internal").ap()

        ident = sb("ident", [P, P])
        eps_ident = sb("eps_ident", [P, P])
        eps_col = sb("eps_col", [P, 1])
        before = sb("before", [P, P], BF16)
        ones = sb("ones", [P, P], BF16)
        minus_half = sb("minus_half", [P, TT])
        expert_no = sb("expert_no", [P, E])
        region = sb("region", [P, E])
        token_no = sb("token_no", [P, TILES], I32)
        w1_sb = sb("w1_sb", [P, H])
        w1_hi = sb("w1_hi", [P, H], F32R)
        w1_lo = sb("w1_lo", [P, H], F32R)
        rms_w_sb = sb("rms_w_sb", [P, H])
        w2_sb = sb("w2_sb", [P, HC, D])
        router_sb = sb("router_sb", [P, E])
        BIAS = H + D
        bias3 = sb("bias3", [3, BIAS])
        bias_rest = sb("bias_rest", [3, 2, BIAS])
        bias_part = sb("bias_part", [3, 3, BIAS], BF16)
        bias_cut = sb("bias_cut", [3, BIAS], BF16)
        bias_sum = sb("bias_sum", [3, 2, BIAS], BF16)
        tokens = sb("tokens", [P, TILES, D])
        adj = sb("adj", [P, 2, TT, N])
        stats1 = sb("stats1", [P, 2, TT, 6])
        mean_var1 = sb("mean_var1", [P, 2, TT, 2])
        var1 = sb("var1", [P, 2, TT])
        rstd1 = sb("rstd1", [P, 2, TT])
        normed = sb("normed", [P, 2, TT, D])
        agg_hi = sb("agg_hi", [P, 2, N], F32R)
        agg_lo = sb("agg_lo", [P, 2, N], F32R)
        squares = sb("squares", [P, TT, H])
        mean_sq = sb("mean_sq", [P, 2, TT])
        mean_sq_eps = sb("mean_sq_eps", [P, 2, TT])
        rms = sb("rms", [P, 2, TT])
        scaled = sb("scaled", [P, 2, TT, H])
        hidden_t = sb("hidden_t", [P, 2, TT, HC, P])
        stats2 = sb("stats2", [P, 2, TT, 6])
        mean_var2 = sb("mean_var2", [P, 2, TT, 2])
        var2 = sb("var2", [P, 2, TT])
        rstd2 = sb("rstd2", [P, 2, TT])
        shift2 = sb("shift2", [P, 2, TT])
        rows = sb("rows", [P, 4, TOP, TT, ROW])
        normed2_t = sb("normed2_t", [P, 2, N])
        logits = sb("logits", [P, 2, TT, E])
        largest = sb("largest", [P, 2, TT, E])
        sorted_logits = sb("sorted_logits", [P, TILES, E])
        order = sb("order", [P, 2, TT, E], U32)
        chosen = sb("chosen", [P, 2, TOP, TT, E])
        mask = sb("mask", [P, 2, TT, E], BF16)
        taken = sb("taken", [P, TILES + 1, E], BF16)
        place = sb("place", [P, 2, TT, E])
        chosen_place = sb("chosen_place", [P, 2, TOP, TT, E])
        slot = sb("slot", [P, 4, TOP * TT], U32)
        gate_exp = sb("gate_exp", [P, TILES, E])
        gate_sum = sb("gate_sum", [P, TILES])
        gate_den = sb("gate_den", [P, 2, TILES])
        gate_inv = sb("gate_inv", [P, TILES])
        gates = sb("gates", [P, TOP, TILES])
        counts = sb("counts", [P, E])
        count_int = sb("count_int", [P, E], I32)
        tile_whole = sb("tile_whole", [P, E, TILES])
        tile_limit = sb("tile_limit", [P, TILES])
        tile_count = sb("tile_count", [P, E])
        tile_end = sb("tile_end", [P, E])
        zeros8 = sb("zeros8", [P, E])
        jump = sb("jump", [P, E])
        tile_no = sb("tile_no", [P, SLOT_TILES])
        passed = sb("passed", [P, 2, SLOT_TILES])
        tile_expert = sb("tile_expert", [P, 2, SLOT_TILES])
        tile_base = sb("tile_base", [P, 2, SLOT_TILES])
        expert_int = sb("expert_int", [P, SLOT_TILES], I32)
        base_int = sb("base_int", [P, SLOT_TILES], I32)
        padding = sb("padding", [P, 2 * E, ROW])
        ew1_sb = sb("ew1_sb", [P, E * EHP])
        ew3_sb = sb("ew3_sb", [P, E * EHP])
        ew1_hi = sb("ew1_hi", [P, E * EHP], F32R)
        ew1_lo = sb("ew1_lo", [P, E * EHP], F32R)
        ew3_hi = sb("ew3_hi", [P, E * EHP], F32R)
        ew3_lo = sb("ew3_lo", [P, E * EHP], F32R)
        ew2_sb = sb("ew2_sb", [HK, E * CHUNKS * D])
        slot_rows = sb("slot_rows", [P, 4, ROW])
        rows_hi = sb("rows_hi", [P, 2, P], F32R)
        rows_lo = sb("rows_lo", [P, 2, P], F32R)
        silu1 = scaled[:, 0, :, 0:EHP]
        prod = scaled[:, 1, :, 0:EHP]
        prod_t = squares[0:HK, :, 0:CHUNKS * P].rearrange("p r (c n) -> p r c n", c=CHUNKS)
        dest = sb("dest", [P, 4, 1], U32)
        zero_int = sb("zero_int", [P, 1], U32)
        result = sb("result", [P, 4, D])
        FG = 4
        picked = ew1_sb[:, 0:2 * TOP * FG * D].rearrange("p (r k t d) -> p r k t d", r=2, k=TOP, t=FG)

        agg_ps = bank("agg_ps", [P, 512])
        hid_ps = [bank(f"hid_ps{t}", [P, 512]) for t in range(TT)]
        hidt_ps = [bank(f"hidt_ps{t}", [P, 512]) for t in range(TT)]
        y_ps = bank("y_ps", [P, 512])
        rowt_ps = bank("rowt_ps", [P, 512])
        route_ps = bank("route_ps", [P, 512])
        h1_ps = [agg_ps, hid_ps[0]]
        h3_ps = [hid_ps[1], hidt_ps[0]]
        prodt_ps = [hidt_ps[1], route_ps]

        s_w1 = sem("w1_loaded"); s_bias = sem("bias_loaded"); s_small = sem("small_loaded"); s_w2 = sem("w2_loaded")
        s_ew1 = sem("ew1_loaded"); s_ew3 = sem("ew3_loaded"); s_ew2 = sem("ew2_loaded")
        s_unit = [sem(f"unit_loaded{r}") for r in range(2)]
        s_mem = sem("constants_set"); s_const = sem("constants_ready")
        s_bcut = sem("bias_steps"); s_w1cut = sem("w1_split"); s_epsid = sem("eps_ident_ready")
        s_adj = sem("adj_ready"); s_st1 = sem("stats1_done"); s_mv1 = sem("mean_var1_done")
        s_var1 = sem("var1_ready"); s_rstd1 = sem("rstd1_ready"); s_normed = sem("normed_ready")
        s_agg = sem("agg_done"); s_agghi = sem("agg_hi_ready"); s_agglo = sem("agg_lo_ready")
        s_hid = sem("hidden_done"); s_sq = sem("squares_done"); s_msq = sem("mean_sq_ready")
        s_rms = sem("rms_ready"); s_scaled = sem("scaled_ready"); s_hidt = sem("hidden_transposed")
        s_silu = sem("silu_ready"); s_y = sem("y_done"); s_x2 = sem("tokens_updated")
        s_st2 = sem("stats2_done"); s_mv2 = sem("mean_var2_done"); s_var2 = sem("var2_ready")
        s_rstd2 = sem("rstd2_ready"); s_shift2 = sem("shift2_ready"); s_row0 = sem("first_rows_ready")
        s_row1 = sem("rows_ready"); s_rowt = sem("rows_transposed"); s_rowtc = sem("normed2_t_ready")
        s_logit = sem("logits_done"); s_route = sem("routing_steps"); s_mask = sem("mask_ready")
        s_rank = sem("rank_done"); s_place = sem("place_read"); s_slot = sem("slot_ready")
        s_sent = [sem(f"rows_sent{r}") for r in range(4)]
        s_cnt = sem("counts_done"); s_tab = sem("table_steps"); s_table = sem("table_ready")
        s_pad = sem("padding_ready"); s_padded = sem("padding_written"); s_cntint = sem("count_int_ready")
        s_gate = sem("gate_steps"); s_gexp = sem("gate_exp_ready")
        s_ehi = sem("expert_hi_ready"); s_elo = sem("expert_lo_ready")
        s_slotrow = [sem(f"slot_rows_loaded{r}") for r in range(4)]
        s_xt = sem("slot_rows_transposed"); s_xhi = sem("rows_hi_ready"); s_xlo = sem("rows_lo_ready")
        s_h1 = sem("h1_done"); s_h3 = sem("h3_done"); s_silu1 = sem("silu1_ready"); s_dest = sem("dest_ready")
        s_prod = sem("prod_ready"); s_prodt = sem("prod_transposed"); s_prodtc = sem("prod_t_ready")
        s_yy = sem("expert_y_done"); s_res = sem("result_ready")
        s_resout = [sem(f"results_sent{r}") for r in range(4)]
        s_picked = [sem(f"picked_loaded{r}") for r in range(2)]
        s_sum1 = sem("first_choice_added"); s_sum2 = sem("second_choice_added")
        s_out = [sem(f"out_written{r}") for r in range(2)]

        G = dict(first=-3, steady=5, bodies=(GRAPHS - 3 - 5) // UNROLL, last=GRAPHS + 3)
        X = dict(first=-1, steady=6, bodies=(SLOT_TILES - 1 - 6) // UNROLL, last=SLOT_TILES + 1)

        block = ctx.enter_context(nc.Block())

        @block.sync
        def _(sp):
            sp.dma_start(bias3[:, :], b1[:, :]).then_inc(s_bias, 16)
            sp.dma_start(w1_sb[:, :], w1).then_inc(s_w1, 16)

            def load_unit(u):
                if positive(u.plus(-1).n):
                    sp.wait_ge(s_agg, u.plus(-1).n)
                sp.dma_start(tokens[:, bass.ds(u.n * TT, TT), :],
                             x.rearrange("(t p) d -> p t d", p=P)[:, bass.ds(u.n * TT, TT), :]
                             ).then_inc(s_unit[u.ring(2)], 16)
                sp.dma_start(adj[:, u.ring(2), :, :],
                             adj_t.rearrange("(b c p) n -> p b c n", p=P, c=TT)[:, bass.ds(u.n, 1), :, :]
                             .rearrange("p b c n -> p (b c) n")
                             ).then_inc(s_unit[u.ring(2)], 16)

            for u in range(4):
                load_unit(Step(0, u))
                if u == 0:
                    sp.dma_start(w2_sb[:, :, :], w2.rearrange("(c p) d -> p c d", p=P)).then_inc(s_w2, 16)
                if u == 3:
                    sp.dma_start(ew1_sb[:, :], ew1).then_inc(s_ew1, 16)
                    sp.dma_start(ew3_sb[:, :], ew3).then_inc(s_ew3, 16)
                    sp.dma_start(ew2_sb[:, :], ew2).then_inc(s_ew2, 16)
            with sp.Fori(1, GRAPHS // UNROLL) as k:
                for q in range(UNROLL):
                    load_unit(Step(k, q))

            sp.wait_ge(s_pad, 1)
            sp.dma_start(expert_rows[E * CAP:E * CAP + E * P, :].rearrange("(b p) r -> p b r", p=P),
                         padding[:, E:2 * E, :]).then_inc(s_padded, 16)
            sp.wait_ge(s_cntint, 1)
            for e in range(E):
                count = sp.value_load(count_int[0:1, e:e + 1], min_val=0, max_val=TOKENS)
                sp.dma_start(expert_rows[bass.ds(count + e * CAP, P), :], padding[:, e, :]).then_inc(s_padded, 16)
            sp.wait_ge(s_padded, 16 * (E + 1))
            for r in range(4):
                sp.wait_ge(s_sent[r], 16 * TOP * TT * (GRAPHS // 4))
            sp.wait_ge(s_table, 1)

            def load_slots(i):
                if positive(i.plus(-3).n):
                    sp.wait_ge(s_xt, i.plus(-3).n)
                    sp.wait_ge(s_dest, i.plus(-3).n)
                base = sp.value_load(base_int[0:1, bass.ds(i.n, 1)], min_val=0, max_val=E * CAP + (E - 1) * P)
                sp.dma_start(slot_rows[:, i.ring(4), :],
                             expert_rows[bass.ds(base, P), :]).then_inc(s_slotrow[i.ring(4)], 16)

            for i in range(4):
                load_slots(Step(0, i))
            with sp.Fori(1, SLOT_TILES // UNROLL) as k:
                for q in range(UNROLL):
                    load_slots(Step(k, q))

            for r in range(4):
                sp.wait_ge(s_resout[r], 16 * (SLOT_TILES // 4))
            STEPS = TILES // FG
            picks = results[0:TOP * TOKENS, :].rearrange("(k t p) d -> p k t d", p=P, k=TOP)
            out_t = out.rearrange("(t p) d -> p t d", p=P)

            def load_picked(g):
                for c in range(TOP):
                    sp.dma_start(picked[:, g.ring(2), c, :, :],
                                 picks[:, c, bass.ds(g.n * FG, FG), :]).then_inc(s_picked[g.ring(2)], 16)

            def store(g):
                sp.wait_ge(s_sum2, g.plus(1).n)
                sp.dma_start(out_t[:, bass.ds(g.n * FG, FG), :],
                             tokens[:, bass.ds(g.n * FG, FG), :]).then_inc(s_out[g.ring(2)], 16)

            load_picked(Step(0, 0))
            load_picked(Step(0, 1))
            with sp.Fori(0, STEPS // UNROLL - 1) as k:
                for q in range(UNROLL):
                    store(Step(k, q))
                    load_picked(Step(k, q + 2))
            for q in range(STEPS - UNROLL, STEPS):
                store(Step(0, q))
                if q + 2 < STEPS:
                    load_picked(Step(0, q + 2))
            for r in range(2):
                sp.wait_ge(s_out[r], 16 * (STEPS // 2))

        @block.gpsimd
        def _(pool):
            pool.memset(ident[:, :], 0.0).then_inc(s_mem, 1)
            pool.memset(before[:, :], 1.0).then_inc(s_mem, 1)
            pool.memset(ones[:, :], 1.0).then_inc(s_const, 1)
            pool.memset(minus_half[:, :], -0.5).then_inc(s_const, 1)
            pool.wait_ge(s_mem, 2)
            pool.affine_select(out=ident[:, :], in_=ident[:, :], compare_op=ALU.not_equal, fill=1.0,
                               base=0, pattern=[[-1, P]], channel_multiplier=1).then_inc(s_const, 1)
            pool.affine_select(out=before[:, :], in_=before[:, :], compare_op=ALU.is_gt, fill=0.0,
                               base=0, pattern=[[1, P]], channel_multiplier=-1).then_inc(s_const, 1)
            pool.iota(expert_no[:, :], pattern=[[1, E]], base=0, channel_multiplier=0,
                      allow_small_or_imprecise_dtypes=True).then_inc(s_const, 1)
            pool.iota(token_no[:, :], pattern=[[P, TILES]], base=0, channel_multiplier=1).then_inc(s_const, 1)
            pool.iota(region[:, :], pattern=[[CAP, E]], base=0, channel_multiplier=0,
                      allow_small_or_imprecise_dtypes=True).then_inc(s_const, 1)
            pool.iota(tile_no[:, :], pattern=[[1, SLOT_TILES]], base=0, channel_multiplier=0,
                      allow_small_or_imprecise_dtypes=True).then_inc(s_const, 1)
            pool.iota(tile_limit[:, :], pattern=[[P, TILES]], base=0, channel_multiplier=0,
                      allow_small_or_imprecise_dtypes=True).then_inc(s_const, 1)
            pool.memset(taken[:, 0, :], 0.0).then_inc(s_const, 1)
            pool.memset(zeros8[:, :], 0.0)
            pool.memset(zero_int[:, :], 0).then_inc(s_const, 1)
            pool.memset(rows[:, :, :, :, D + 1:ROW], 0.0).then_inc(s_const, 1)
            pool.memset(padding[:, :, :], 0.0).then_inc(s_mem, 1)
            pool.wait_ge(s_mem, 3)
            pool.iota(padding[:, :, D].bitcast(I32), pattern=[[P, 2 * E]], base=TOP * TOKENS,
                      channel_multiplier=1).then_inc(s_pad, 1)

            def rstd1_of(u):
                pool.wait_ge(s_var1, u.plus(1).n)
                r = u.ring(2)
                if positive(u.plus(-1).n):
                    pool.wait_ge(s_normed, u.plus(-1).n)
                pool.tensor_tensor(rstd1[:, r, :], var1[:, r, :], minus_half[:, :], ALU.pow).then_inc(s_rstd1, 1)

            def rms_of(u):
                pool.wait_ge(s_msq, u.plus(1).n)
                r = u.ring(2)
                if positive(u.plus(-1).n):
                    pool.wait_ge(s_scaled, u.plus(-1).n * TT)
                pool.tensor_tensor(rms[:, r, :], mean_sq_eps[:, r, :], minus_half[:, :], ALU.pow).then_inc(s_rms, 1)

            def rstd2_of(u):
                sent = u.plus(-3)
                if sent.within(GRAPHS):
                    pool.wait_ge(s_slot, sent.plus(1).n)
                    pool.wait_ge(s_row1, sent.plus(1).n)
                if not u.within(GRAPHS):
                    return
                pool.wait_ge(s_var2, u.plus(1).n)
                r = u.ring(2)
                if positive(u.plus(-1).n):
                    pool.wait_ge(s_row0, u.plus(-1).n)
                pool.tensor_tensor(rstd2[:, r, :], var2[:, r, :], minus_half[:, :], ALU.pow).then_inc(s_rstd2, 1)

            def send(u, c):
                r = u.ring(4)
                for t in range(TT):
                    pool.indirect_dma_start(
                        out=expert_rows, out_offset=bass.IndirectOffsetOnAxis(
                            ap=slot[:, r, c * TT + t:c * TT + t + 1], axis=0),
                        in_=rows[:, r, c, t, :], in_offset=None).then_inc(s_sent[r], 16)

            def step(j):
                rstd2_of(j.plus(-1))
                if j.plus(-4).within(GRAPHS):
                    send(j.plus(-4), 0)
                if j.plus(3).within(GRAPHS):
                    rstd1_of(j.plus(3))
                if j.plus(1).within(GRAPHS):
                    rms_of(j.plus(1))
                if j.plus(-4).within(GRAPHS):
                    send(j.plus(-4), 1)

            pool.wait_ge(s_const, 4)
            run_steps(pool, G["first"], G["steady"] + 1, G["bodies"] - 1, G["last"], step)

            def destinations(i):
                q = i.ring(4)
                pool.wait_ge(s_slotrow[q], i.turn(4) * 16 + 16)
                if positive(i.turn(4)):
                    pool.wait_ge(s_resout[q], i.turn(4) * 16)
                pool.tensor_tensor(dest[:, q, :], slot_rows[:, q, D:D + 1].bitcast(U32), zero_int[:, :],
                                   ALU.add).then_inc(s_dest, 1)

            def send_result(i, ahead):
                pool.wait_ge(s_res, i.plus(1).n)
                pool.wait_ge(s_dest, i.plus(1).n)
                if ahead.within(SLOT_TILES):
                    destinations(ahead)
                r = i.ring(4)
                pool.indirect_dma_start(
                    out=results, out_offset=bass.IndirectOffsetOnAxis(ap=dest[:, r, :], axis=0),
                    in_=result[:, r, :], in_offset=None).then_inc(s_resout[r], 16)

            def expert_step(i):
                if i.within(SLOT_TILES):
                    send_result(i, i.plus(2))
                else:
                    destinations(i.plus(2))

            run_steps(pool, -2, 4, (SLOT_TILES - 2 - 4) // UNROLL, SLOT_TILES - 1, expert_step)

        @block.scalar
        def _(act):
            act.dma_start(rms_w_sb[:, :], rms_w).then_inc(s_small, 16)
            act.dma_start(router_sb[:, :], router_t).then_inc(s_small, 16)
            act.dma_start(eps_col[:, :], eps).then_inc(s_small, 16)

            def agg_high(u):
                r = u.ring(2)
                act.wait_ge(s_agg, u.plus(1).n)
                if positive(u.plus(-1).n):
                    act.wait_ge(s_hid, u.plus(-1).n * TT)
                act.activation(agg_hi[:, r, :], agg_ps[:, 0:N], ACT.Copy).then_inc(s_agghi, 1)

            def silu_of(u):
                r = u.ring(2)
                for t in range(TT):
                    act.wait_ge(s_hidt, u.n * TT + t + 1)
                    if t == 0 and positive(u.plus(-1).n):
                        act.wait_ge(s_y, u.plus(-1).n)
                    act.activation(hidden_t[:, r, t, :, :].rearrange("p c n -> p (c n)"), hidt_ps[t][:, :],
                                   ACT.Silu).then_inc(s_silu, 1)

            def normed_rows(u):
                r = u.ring(2)
                act.wait_ge(s_shift2, u.plus(1).n)
                if positive(u.turn(4)):
                    act.wait_ge(s_sent[u.ring(4)], u.turn(4) * (16 * TOP * TT))
                for t in range(TT):
                    ins = act.activation(rows[:, u.ring(4), 0, t, 0:D], tokens[:, u.n * TT + t, :], ACT.Identity,
                                         bias=shift2[:, r, t:t + 1], scale=rstd2[:, r, t:t + 1])
                ins.then_inc(s_row0, 1)

            def squares_of(u):
                r = u.ring(2)
                if positive(u.plus(-1).n):
                    act.wait_ge(s_msq, u.plus(-1).n)
                for t in range(TT):
                    act.wait_ge(s_hid, u.n * TT + t + 1)
                    if positive(u.n):
                        act.wait_ge(s_sq, u.n * TT + t - 1)
                    act.activation(squares[:, t, :], hid_ps[t][:, :], ACT.Square, scale=float(H) ** -0.5,
                                   accum_out=mean_sq[:, r, t:t + 1]).then_inc(s_sq, 1)

            def rows_t(u):
                r = u.ring(2)
                act.wait_ge(s_rowt, u.plus(1).n)
                if positive(u.plus(-1).n):
                    act.wait_ge(s_logit, u.plus(-1).n)
                act.activation(normed2_t[:, r, :], rowt_ps[:, 0:N], ACT.Copy).then_inc(s_rowtc, 1)

            def step(j):
                if j.plus(2).within(GRAPHS):
                    agg_high(j.plus(2))
                if j.within(GRAPHS):
                    silu_of(j)
                if j.plus(-1).within(GRAPHS):
                    normed_rows(j.plus(-1))
                if j.plus(1).within(GRAPHS):
                    squares_of(j.plus(1))
                if j.plus(-2).within(GRAPHS):
                    rows_t(j.plus(-2))

            act.wait_ge(s_const, 12)
            run_steps(act, G["first"], G["steady"], G["bodies"], G["last"], step)

            act.wait_ge(s_ew1, 16)
            act.activation(ew1_hi[:, :], ew1_sb[:, :], ACT.Copy).then_inc(s_ehi, 1)
            act.wait_ge(s_ew3, 16)
            act.activation(ew3_hi[:, :], ew3_sb[:, :], ACT.Copy).then_inc(s_ehi, 1)

            def rows_high(i):
                r = i.ring(2)
                act.wait_ge(s_xt, i.plus(1).n)
                if positive(i.plus(-1).n):
                    act.wait_ge(s_h3, i.plus(-1).n)
                act.activation(rows_hi[:, r, :], rowt_ps[:, 0:P], ACT.Copy).then_inc(s_xhi, 1)

            def silu_h1(i):
                r = i.ring(2)
                act.wait_ge(s_h1, i.plus(1).n)
                if positive(i.plus(-1).n):
                    act.wait_ge(s_prod, i.plus(-1).n)
                act.activation(silu1[:, r, :], h1_ps[r][:, 0:EHP], ACT.Silu).then_inc(s_silu1, 1)

            def prod_transposed(i):
                r = i.ring(2)
                act.wait_ge(s_prodt, i.plus(1).n)
                if positive(i.plus(-1).n):
                    act.wait_ge(s_yy, i.plus(-1).n)
                act.activation(prod_t[:, r, :, :].rearrange("p c n -> p (c n)"), prodt_ps[r][0:HK, 0:CHUNKS * P],
                               ACT.Copy).then_inc(s_prodtc, 1)

            def expert_step(i):
                if i.plus(1).within(SLOT_TILES):
                    rows_high(i.plus(1))
                if i.within(SLOT_TILES):
                    silu_h1(i)
                if i.plus(-1).within(SLOT_TILES):
                    prod_transposed(i.plus(-1))

            run_steps(act, X["first"], X["steady"], X["bodies"], X["last"], expert_step)

            act.wait_ge(s_gate, 1)
            act.activation(gate_exp[:, :, :], gate_exp[:, :, :], ACT.Exp).then_inc(s_gexp, 1)

        @block.tensor
        def _(pe):
            def sum_neighbours(u):
                r = u.ring(2)
                pe.wait_ge(s_normed, u.plus(1).n)
                pe.wait_ge(s_adj, u.plus(1).n)
                if positive(u.n):
                    pe.wait_ge(s_agglo, u.n)
                for c in range(TT):
                    ins = pe.matmul(agg_ps[:, 0:N], normed[:, r, c, :], adj[:, r, c, :], start=(c == 0), stop=(c == TT - 1))
                ins.then_inc(s_agg, 1)

            def transpose_hidden(u):
                for t in range(TT):
                    pe.wait_ge(s_scaled, u.n * TT + t + 1)
                    if positive(u.n):
                        pe.wait_ge(s_silu, u.n * TT + t - 1)
                    for c in range(HC):
                        ins = pe.transpose(hidt_ps[t][:, c * P:(c + 1) * P],
                                           scaled[:, u.ring(2), t, c * P:(c + 1) * P], ident[:, :])
                    ins.then_inc(s_hidt, 1)

            def first_product(u):
                r = u.ring(2)
                pe.wait_ge(s_agglo, u.plus(1).n)
                for t in range(TT):
                    if positive(u.n):
                        pe.wait_ge(s_scaled, u.n * TT + t - 1)
                    hi, lo = agg_hi[:, r, t * P:(t + 1) * P], agg_lo[:, r, t * P:(t + 1) * P]
                    pe.matmul(hid_ps[t][:, :], ones[0:3, :], bias_cut[:, 0:H], start=True, stop=False)
                    pe.matmul(hid_ps[t][:, :], lo, w1_hi[:, :], start=False, stop=False)
                    pe.matmul(hid_ps[t][:, :], hi, w1_lo[:, :], start=False, stop=False)
                    pe.matmul(hid_ps[t][:, :], hi, w1_hi[:, :], start=False, stop=True).then_inc(s_hid, 1)

            def second_product(u):
                if positive(u.n):
                    pe.wait_ge(s_x2, u.n)
                for t in range(TT):
                    pe.wait_ge(s_silu, u.n * TT + t + 1)
                    pe.matmul(y_ps[:, t * D:(t + 1) * D], ones[0:3, :], bias_cut[:, H:H + D], start=True, stop=False)
                    for c in range(HC):
                        ins = pe.matmul(y_ps[:, t * D:(t + 1) * D], hidden_t[:, u.ring(2), t, c, :], w2_sb[:, c, :],
                                        start=False, stop=(c == HC - 1))
                ins.then_inc(s_y, 1)

            def transpose_rows(u):
                pe.wait_ge(s_row0, u.plus(1).n)
                if positive(u.n):
                    pe.wait_ge(s_rowtc, u.n)
                for t in range(TT):
                    ins = pe.transpose(rowt_ps[:, t * P:(t + 1) * P], rows[:, u.ring(4), 0, t, 0:D], ident[:, :])
                ins.then_inc(s_rowt, 1)

            def router(u):
                pe.wait_ge(s_rowtc, u.plus(1).n)
                if positive(u.n):
                    pe.wait_ge(s_place, u.n)
                for t in range(TT):
                    ins = pe.matmul(route_ps[:, t * E:(t + 1) * E], normed2_t[:, u.ring(2), t * P:(t + 1) * P],
                                    router_sb[:, :], start=True, stop=True)
                ins.then_inc(s_logit, 1)

            def rank(u):
                pe.wait_ge(s_mask, u.plus(1).n)
                for t in range(TT):
                    part = route_ps[:, 64 + t * E:64 + (t + 1) * E]
                    pe.matmul(part, before[:, :], mask[:, u.ring(2), t, :], start=True, stop=False)
                    ins = pe.matmul(part, ones[:, :], taken[:, u.n * TT + t, :], start=False, stop=True)
                ins.then_inc(s_rank, 1)

            def step(j):
                if j.plus(2).within(GRAPHS):
                    sum_neighbours(j.plus(2))
                if j.within(GRAPHS):
                    transpose_hidden(j)
                if j.plus(-3).within(GRAPHS):
                    rank(j.plus(-3))
                if j.plus(1).within(GRAPHS):
                    first_product(j.plus(1))
                if j.plus(-2).within(GRAPHS):
                    transpose_rows(j.plus(-2))
                if j.within(GRAPHS):
                    second_product(j)
                if j.plus(-2).within(GRAPHS):
                    router(j.plus(-2))

            pe.wait_ge(s_const, 12)
            pe.wait_ge(s_small, 48)
            pe.wait_ge(s_w2, 16)
            pe.wait_ge(s_w1cut, 2)
            pe.wait_ge(s_bcut, 9)
            run_steps(pe, G["first"], G["steady"], G["bodies"], G["last"], step)

            pe.wait_ge(s_place, GRAPHS)
            pe.matmul(route_ps[:, 0:E], ones[:, :], taken[:, TILES, :], start=True, stop=True).then_inc(s_cnt, 1)

            pe.wait_ge(s_ew2, 16)
            pe.wait_ge(s_elo, 2)
            pe.wait_ge(s_table, 1)

            def transpose_slots(i):
                pe.wait_ge(s_slotrow[i.ring(4)], i.turn(4) * 16 + 16)
                if positive(i.n):
                    pe.wait_ge(s_xlo, i.n)
                pe.transpose(rowt_ps[:, 0:P], slot_rows[:, i.ring(4), 0:D], ident[:, :]).then_inc(s_xt, 1)

            def up(i, expert):
                r = i.ring(2)
                pe.wait_ge(s_xlo, i.plus(1).n)
                if positive(i.plus(-1).n):
                    pe.wait_ge(s_prod, i.plus(-1).n)
                at = bass.ds(expert * EHP, EHP)
                for ps, w_hi, w_lo, done in ((h1_ps[r], ew1_hi, ew1_lo, s_h1), (h3_ps[r], ew3_hi, ew3_lo, s_h3)):
                    pe.matmul(ps[:, 0:EHP], rows_lo[:, r, :], w_hi[:, at], start=True, stop=False)
                    pe.matmul(ps[:, 0:EHP], rows_hi[:, r, :], w_lo[:, at], start=False, stop=False)
                    pe.matmul(ps[:, 0:EHP], rows_hi[:, r, :], w_hi[:, at], start=False, stop=True).then_inc(done, 1)

            def down(i, expert):
                r = i.ring(2)
                pe.wait_ge(s_prodtc, i.plus(1).n)
                if positive(i.n):
                    pe.wait_ge(s_res, i.n)
                for c in range(CHUNKS):
                    ins = pe.matmul(y_ps[:, 0:D], prod_t[:, r, c, :], ew2_sb[:, bass.ds((expert * CHUNKS + c) * D, D)],
                                    start=(c == 0), stop=(c == CHUNKS - 1))
                ins.then_inc(s_yy, 1)

            def transpose_prod(i):
                r = i.ring(2)
                pe.wait_ge(s_prod, i.plus(1).n)
                if positive(i.plus(-1).n):
                    pe.wait_ge(s_prodtc, i.plus(-1).n)
                for c in range(CHUNKS):
                    ins = pe.transpose(prodt_ps[r][0:HK, c * P:(c + 1) * P], prod[:, r, c * HK:(c + 1) * HK], ident[:, :])
                ins.then_inc(s_prodt, 1)

            def expert_of(i):
                return pe.value_load(expert_int[0:1, bass.ds(i.n, 1)], min_val=0, max_val=E - 1)

            def expert_step(i):
                if i.plus(1).within(SLOT_TILES):
                    transpose_slots(i.plus(1))
                if i.within(SLOT_TILES):
                    up(i, expert_of(i))
                if i.plus(-2).within(SLOT_TILES):
                    down(i.plus(-2), expert_of(i.plus(-2)))
                if i.plus(-1).within(SLOT_TILES):
                    transpose_prod(i.plus(-1))

            run_steps(pe, X["first"], X["steady"], X["bodies"], X["last"], expert_step)

        @block.vector
        def _(dve):
            dve.wait_ge(s_w1, 16)
            dve.tensor_copy(w1_hi[:, :], w1_sb[:, :]).then_inc(s_w1cut, 1)
            dve.wait_ge(s_w1cut, 1)
            dve.tensor_tensor(w1_lo[:, :], w1_sb[:, :], w1_hi[:, :].bitcast(F32), ALU.subtract).then_inc(s_w1cut, 1)
            dve.wait_ge(s_bias, 16)
            dve.tensor_copy(bias_part[:, 0, :], bias3[:, :]).then_inc(s_bcut, 1)
            dve.wait_ge(s_bcut, 1)
            dve.tensor_tensor(bias_rest[:, 0, :], bias3[:, :], bias_part[:, 0, :], ALU.subtract).then_inc(s_bcut, 1)
            dve.wait_ge(s_bcut, 2)
            dve.tensor_copy(bias_part[:, 1, :], bias_rest[:, 0, :]).then_inc(s_bcut, 1)
            dve.wait_ge(s_bcut, 3)
            dve.tensor_tensor(bias_rest[:, 1, :], bias_rest[:, 0, :], bias_part[:, 1, :], ALU.subtract).then_inc(s_bcut, 1)
            dve.wait_ge(s_bcut, 4)
            dve.tensor_copy(bias_part[:, 2, :], bias_rest[:, 1, :]).then_inc(s_bcut, 1)
            dve.wait_ge(s_const, 12)
            dve.wait_ge(s_bcut, 5)
            dve.tensor_scalar(bias_sum[:, 0, :], bias_part[:, 0, :], ident[0:3, 0:1], None, ALU.mult).then_inc(s_bcut, 1)
            dve.wait_ge(s_bcut, 6)
            dve.scalar_tensor_tensor(out=bias_sum[:, 1, :], in0=bias_part[:, 1, :], scalar=ident[0:3, 1:2],
                                     in1=bias_sum[:, 0, :], op0=ALU.mult, op1=ALU.add).then_inc(s_bcut, 1)
            dve.wait_ge(s_bcut, 7)
            dve.scalar_tensor_tensor(out=bias_cut[:, :], in0=bias_part[:, 2, :], scalar=ident[0:3, 2:3],
                                     in1=bias_sum[:, 1, :], op0=ALU.mult, op1=ALU.add).then_inc(s_bcut, 1)
            dve.wait_ge(s_small, 48)
            dve.tensor_scalar(eps_ident[:, :], ident[:, :], eps_col[:, 0:1], None, ALU.mult).then_inc(s_bcut, 1)
            dve.wait_ge(s_bcut, 9)

            def normalise1(u):
                r = u.ring(2)
                dve.wait_ge(s_rstd1, u.plus(1).n)
                if positive(u.plus(-1).n):
                    dve.wait_ge(s_agg, u.plus(-1).n)
                for t in range(TT):
                    ins = dve.tensor_scalar(normed[:, r, t, :], tokens[:, u.n * TT + t, :], mean_var1[:, r, t, 0:1],
                                            rstd1[:, r, t:t + 1], ALU.subtract, ALU.mult)
                ins.then_inc(s_normed, 1)

            def agg_low(u):
                r = u.ring(2)
                dve.wait_ge(s_agghi, u.plus(1).n)
                if positive(u.plus(-1).n):
                    dve.wait_ge(s_hid, u.plus(-1).n * TT)
                dve.tensor_tensor(agg_lo[:, r, :], agg_ps[:, 0:N], agg_hi[:, r, :].bitcast(F32),
                                  ALU.subtract).then_inc(s_agglo, 1)

            def mean_square(u):
                r = u.ring(2)
                dve.wait_ge(s_sq, u.n * TT + TT)
                dve.tensor_scalar(mean_sq_eps[:, r, :], mean_sq[:, r, :], RMS_EPS, None, ALU.add).then_inc(s_msq, 1)

            def scale_hidden(u):
                r = u.ring(2)
                dve.wait_ge(s_rms, u.plus(1).n)
                if positive(u.plus(-1).n):
                    dve.wait_ge(s_hidt, u.plus(-1).n * TT)
                for t in range(TT):
                    dve.scalar_tensor_tensor(out=scaled[:, r, t, :], in0=hid_ps[t][:, :], scalar=rms[:, r, t:t + 1],
                                             in1=rms_w_sb[:, :], op0=ALU.mult, op1=ALU.mult).then_inc(s_scaled, 1)

            def shift_of(u):
                r = u.ring(2)
                dve.wait_ge(s_rstd2, u.plus(1).n)
                if positive(u.plus(-1).n):
                    dve.wait_ge(s_row0, u.plus(-1).n)
                dve.scalar_tensor_tensor(out=shift2[:, r, :], in0=mean_var2[:, r, :, 0], scalar=-1.0,
                                         in1=rstd2[:, r, :], op0=ALU.mult, op1=ALU.mult).then_inc(s_shift2, 1)

            def finish_rows(u):
                q = u.ring(4)
                dve.wait_ge(s_row0, u.plus(1).n)
                if positive(u.turn(4)):
                    dve.wait_ge(s_sent[q], u.turn(4) * (16 * TOP * TT))
                dve.tensor_copy(rows[:, q, 1, :, 0:D], rows[:, q, 0, :, 0:D])
                for c in range(TOP):
                    ins = dve.tensor_scalar(rows[:, q, c, :, D].bitcast(I32), token_no[:, bass.ds(u.n * TT, TT)],
                                            float(c * TOKENS), None, ALU.add)
                ins.then_inc(s_row1, 1)

            def statistics(fresh, ended, routed):
                f, d, r = fresh.ring(2), ended.ring(2), routed.ring(2)
                is_fresh, is_ended, is_routed = (u.within(GRAPHS) for u in (fresh, ended, routed))
                if is_ended:
                    dve.wait_ge(s_y, ended.plus(1).n)
                    mine = tokens[:, bass.ds(ended.n * TT, TT), :]
                    dve.tensor_tensor(mine, y_ps[:, 0:TT * D].rearrange("p (t d) -> p t d", t=TT), mine,
                                      ALU.add).then_inc(s_x2, 1)
                if is_routed:
                    dve.wait_ge(s_logit, routed.plus(1).n)
                    dve.tensor_copy(logits[:, r, :, :].rearrange("p t e -> p (t e)"),
                                    route_ps[:, 0:TT * E]).then_inc(s_route, 1)
                if is_ended:
                    dve.wait_ge(s_x2, ended.plus(1).n)
                if is_routed:
                    dve.wait_ge(s_route, routed.n * 6 + 1)
                if is_fresh:
                    dve.wait_ge(s_unit[f], fresh.turn(2) * 32 + 32)
                    for c in range(TT):
                        part = adj[:, f, c, c * P:(c + 1) * P]
                        ins = dve.tensor_tensor(part, part, eps_ident[:, :], ALU.add)
                    ins.then_inc(s_adj, 1)
                    for t in range(TT):
                        ins = dve.bn_stats(stats1[:, f, t, :], tokens[:, fresh.n * TT + t, :])
                    ins.then_inc(s_st1, 1)
                if is_ended:
                    for t in range(TT):
                        ins = dve.bn_stats(stats2[:, d, t, :], tokens[:, ended.n * TT + t, :])
                    ins.then_inc(s_st2, 1)
                if is_routed:
                    for t in range(TT):
                        ins = dve.max(largest[:, r, t, :], logits[:, r, t, :])
                    ins.then_inc(s_route, 1)
                if is_fresh:
                    dve.wait_ge(s_st1, fresh.plus(1).n)
                if is_ended:
                    dve.wait_ge(s_st2, ended.plus(1).n)
                if is_routed:
                    dve.wait_ge(s_route, routed.n * 6 + 2)
                    dve.tensor_copy(sorted_logits[:, bass.ds(routed.n * TT, TT), :], largest[:, r, :, :])
                if is_fresh:
                    for t in range(TT):
                        ins = dve.bn_aggr(mean_var1[:, f, t, :], stats1[:, f, t, :])
                    ins.then_inc(s_mv1, 1)
                if is_ended:
                    for t in range(TT):
                        ins = dve.bn_aggr(mean_var2[:, d, t, :], stats2[:, d, t, :])
                    ins.then_inc(s_mv2, 1)
                if is_routed:
                    for t in range(TT):
                        ins = dve.max_index(order[:, r, t, :], largest[:, r, t, :], logits[:, r, t, :])
                    ins.then_inc(s_route, 1)
                if is_ended:
                    dve.wait_ge(s_mv2, ended.plus(1).n)
                    dve.tensor_scalar(var2[:, d, :], mean_var2[:, d, :, 1], LN_EPS, None, ALU.add).then_inc(s_var2, 1)
                if is_fresh:
                    dve.wait_ge(s_mv1, fresh.plus(1).n)
                    dve.tensor_scalar(var1[:, f, :], mean_var1[:, f, :, 1], LN_EPS, None, ALU.add).then_inc(s_var1, 1)

            def choose(u):
                r = u.ring(2)
                dve.wait_ge(s_route, u.n * 6 + 3)
                for c in range(TOP):
                    ins = dve.tensor_tensor(chosen[:, r, c, :, :], expert_no[:, :].unsqueeze(1).to_broadcast([P, TT, E]),
                                            order[:, r, :, c:c + 1].to_broadcast([P, TT, E]), ALU.is_equal)
                ins.then_inc(s_route, 1)
                dve.wait_ge(s_route, u.n * 6 + 4)
                if positive(u.plus(-1).n):
                    dve.wait_ge(s_rank, u.plus(-1).n)
                dve.tensor_tensor(mask[:, r, :, :], chosen[:, r, 0, :, :], chosen[:, r, 1, :, :],
                                  ALU.add).then_inc(s_route, 1)
                dve.wait_ge(s_route, u.n * 6 + 5)
                dve.tensor_tensor(taken[:, u.n * TT + 1, :], taken[:, u.n * TT, :], mask[:, r, 0, :],
                                  ALU.add).then_inc(s_route, 1)
                dve.wait_ge(s_route, u.n * 6 + 6)
                dve.tensor_tensor(taken[:, u.n * TT + 2, :], taken[:, u.n * TT + 1, :], mask[:, r, 1, :],
                                  ALU.add).then_inc(s_mask, 1)

            def slots_of(u):
                r, q = u.ring(2), u.ring(4)
                dve.wait_ge(s_rank, u.plus(1).n)
                dve.tensor_tensor(place[:, r, :, :], route_ps[:, 64:64 + TT * E].rearrange("p (t e) -> p t e", t=TT),
                                  region[:, :].unsqueeze(1).to_broadcast([P, TT, E]), ALU.add).then_inc(s_place, 1)
                dve.wait_ge(s_place, u.plus(1).n)
                for c in range(TOP):
                    ins = dve.tensor_tensor(chosen_place[:, r, c, :, :], chosen[:, r, c, :, :], place[:, r, :, :], ALU.mult)
                ins.then_inc(s_tab, 1)
                dve.wait_ge(s_tab, u.plus(1).n)
                if positive(u.turn(4)):
                    dve.wait_ge(s_sent[q], u.turn(4) * (16 * TOP * TT))
                with nc.allow_low_precision(reason="whole numbers below 2**24, added in float32: exact"):
                    dve.tensor_reduce(slot[:, q, :].rearrange("p (c t) -> p c t", c=TOP),
                                      chosen_place[:, r, :, :, :], AX.X, ALU.add).then_inc(s_slot, 1)

            def step(j):
                statistics(j.plus(3), j.plus(-1), j.plus(-3))
                if j.plus(-3).within(GRAPHS):
                    choose(j.plus(-3))
                if j.plus(2).within(GRAPHS):
                    agg_low(j.plus(2))
                if j.plus(-1).within(GRAPHS):
                    shift_of(j.plus(-1))
                if j.plus(-3).within(GRAPHS):
                    slots_of(j.plus(-3))
                if j.plus(3).within(GRAPHS):
                    normalise1(j.plus(3))
                if j.plus(-1).within(GRAPHS):
                    finish_rows(j.plus(-1))
                if j.plus(1).within(GRAPHS):
                    mean_square(j.plus(1))
                    scale_hidden(j.plus(1))

            run_steps(dve, G["first"], G["steady"], G["bodies"], G["last"], step)

            done = GRAPHS
            dve.wait_ge(s_cnt, 1)
            dve.tensor_copy(counts[:, :], route_ps[:, 0:E]).then_inc(s_tab, 1)
            dve.wait_ge(s_tab, done + 1)
            dve.tensor_copy(count_int[:, :], counts[:, :]).then_inc(s_cntint, 1)
            dve.tensor_tensor(tile_whole[:, :, :], counts[:, :].unsqueeze(2).to_broadcast([P, E, TILES]),
                              tile_limit[:, :].unsqueeze(1).to_broadcast([P, E, TILES]), ALU.is_gt).then_inc(s_tab, 1)
            dve.wait_ge(s_tab, done + 2)
            dve.tensor_reduce(tile_count[:, :], tile_whole[:, :, :], AX.X, ALU.add).then_inc(s_tab, 1)
            dve.wait_ge(s_tab, done + 3)
            dve.tensor_tensor_scan(tile_end[:, :], tile_count[:, :], zeros8[:, :], 0.0, ALU.add,
                                   ALU.add).then_inc(s_tab, 1)
            dve.tensor_scalar(jump[:, :], tile_count[:, :], float(-P), float(CAP), ALU.mult, ALU.add).then_inc(s_tab, 1)
            dve.tensor_scalar(tile_base[:, 1, :], tile_no[:, :], float(P), None, ALU.mult).then_inc(s_tab, 1)
            dve.wait_ge(s_tab, done + 6)
            done += 6
            for e in range(E):
                dve.tensor_scalar(passed[:, e % 2, :], tile_no[:, :], tile_end[:, e:e + 1], None,
                                  ALU.is_ge).then_inc(s_tab, 1)
                dve.wait_ge(s_tab, done + 1)
                if e == 0:
                    ins = dve.tensor_copy(tile_expert[:, 0, :], passed[:, 0, :])
                elif e < E - 1:
                    ins = dve.tensor_tensor(tile_expert[:, e % 2, :], tile_expert[:, 1 - e % 2, :],
                                            passed[:, e % 2, :], ALU.add)
                dve.scalar_tensor_tensor(out=tile_base[:, e % 2, :], in0=passed[:, e % 2, :], scalar=jump[:, e:e + 1],
                                         in1=tile_base[:, 1 - e % 2, :], op0=ALU.mult, op1=ALU.add).then_inc(s_tab, 1)
                dve.wait_ge(s_tab, done + 2)
                done += 2
            dve.tensor_copy(expert_int[:, :], tile_expert[:, (E - 2) % 2, :])
            dve.tensor_copy(base_int[:, :], tile_base[:, (E - 1) % 2, :]).then_inc(s_table, 1)

            dve.wait_ge(s_ehi, 1)
            dve.tensor_tensor(ew1_lo[:, :], ew1_sb[:, :], ew1_hi[:, :].bitcast(F32), ALU.subtract).then_inc(s_elo, 1)
            dve.wait_ge(s_ehi, 2)
            dve.tensor_tensor(ew3_lo[:, :], ew3_sb[:, :], ew3_hi[:, :].bitcast(F32), ALU.subtract).then_inc(s_elo, 1)

            def rows_low(i):
                r = i.ring(2)
                dve.wait_ge(s_xhi, i.plus(1).n)
                if positive(i.plus(-1).n):
                    dve.wait_ge(s_h3, i.plus(-1).n)
                dve.tensor_tensor(rows_lo[:, r, :], rowt_ps[:, 0:P], rows_hi[:, r, :].bitcast(F32),
                                  ALU.subtract).then_inc(s_xlo, 1)

            def product(i):
                r = i.ring(2)
                dve.wait_ge(s_silu1, i.plus(1).n)
                dve.wait_ge(s_h3, i.plus(1).n)
                if positive(i.plus(-1).n):
                    dve.wait_ge(s_prodt, i.plus(-1).n)
                dve.tensor_tensor(prod[:, r, :], h3_ps[r][:, 0:EHP], silu1[:, r, :], ALU.mult).then_inc(s_prod, 1)

            def keep_result(i):
                dve.wait_ge(s_yy, i.plus(1).n)
                if positive(i.turn(4)):
                    dve.wait_ge(s_resout[i.ring(4)], i.turn(4) * 16)
                dve.tensor_copy(result[:, i.ring(4), :], y_ps[:, 0:D]).then_inc(s_res, 1)

            def expert_step(i):
                if i.plus(1).within(SLOT_TILES):
                    rows_low(i.plus(1))
                if i.plus(-2).within(SLOT_TILES):
                    keep_result(i.plus(-2))
                if i.within(SLOT_TILES):
                    product(i)

            run_steps(dve, X["first"], X["steady"], X["bodies"], X["last"], expert_step)

            dve.tensor_tensor(gate_exp[:, :, :], sorted_logits[:, :, :],
                              sorted_logits[:, :, 0:1].to_broadcast([P, TILES, E]), ALU.subtract).then_inc(s_gate, 1)
            dve.wait_ge(s_gexp, 1)
            dve.tensor_reduce(gate_sum[:, :], gate_exp[:, :, :], AX.X, ALU.add)
            dve.tensor_tensor(gate_den[:, 0, :], gate_exp[:, :, 0], gate_exp[:, :, 1], ALU.add).then_inc(s_gate, 1)
            dve.wait_ge(s_gate, 2)
            dve.scalar_tensor_tensor(out=gate_den[:, 1, :], in0=gate_sum[:, :], scalar=GATE_EPS, in1=gate_den[:, 0, :],
                                     op0=ALU.mult, op1=ALU.add).then_inc(s_gate, 1)
            dve.wait_ge(s_gate, 3)
            dve.reciprocal(gate_inv[:, :], gate_den[:, 1, :]).then_inc(s_gate, 1)
            dve.wait_ge(s_gate, 4)
            for c in range(TOP):
                ins = dve.tensor_tensor(gates[:, c, :], gate_exp[:, :, c], gate_inv[:, :], ALU.mult)
            ins.then_inc(s_gate, 1)
            dve.wait_ge(s_gate, 5)

            def add_choices(g):
                r = g.ring(2)
                dve.wait_ge(s_picked[r], g.turn(2) * 32 + 32)
                for c, done in ((0, s_sum1), (1, s_sum2)):
                    for t in range(FG):
                        mine = tokens[:, g.n * FG + t, :]
                        ins = dve.scalar_tensor_tensor(
                            out=mine, in0=picked[:, r, c, t, :], scalar=gates[:, c, bass.ds(g.n * FG + t, 1)],
                            in1=mine, op0=ALU.mult, op1=ALU.add)
                    ins.then_inc(done, 1)
                    dve.wait_ge(done, g.plus(1).n)

            with dve.Fori(0, TILES // FG // UNROLL) as k:
                for q in range(UNROLL):
                    add_choices(Step(k, q))


def kernel(x, adj, L0_gnn_epsilon, L0_gnn_W1, L0_gnn_b1, L0_gnn_rms_weight, L0_gnn_W2, L0_gnn_b2,
           L0_ffn_router_w, L0_ffn_w1, L0_ffn_w2, L0_ffn_w3):
    import numpy as np
    from concourse import bacc
    from concourse.bass_utils import run_bass_kernel_spmd

    def up_weights(w):
        padded = np.zeros((D, E, EHP), w.dtype)
        padded[:, :, :EH] = np.transpose(w, (2, 0, 1))
        return padded.reshape(D, E * EHP)

    def down_weights(w):
        padded = np.zeros((E, EHP, D), w.dtype)
        padded[:, :EH] = np.transpose(w, (0, 2, 1))
        return np.transpose(padded.reshape(E, CHUNKS, HK, D), (2, 0, 1, 3)).reshape(HK, E * CHUNKS * D)

    a = {k: np.asarray(v) for k, v in dict(
        x=x, adj=adj, eps=L0_gnn_epsilon, w1=L0_gnn_W1, b1=L0_gnn_b1, rms_w=L0_gnn_rms_weight, w2=L0_gnn_W2,
        b2=L0_gnn_b2, router=L0_ffn_router_w, ew1=L0_ffn_w1, ew2=L0_ffn_w2, ew3=L0_ffn_w3).items()}
    arrays = dict(
        x=a["x"].reshape(TOKENS, D),
        adj_t=np.transpose(a["adj"], (0, 2, 1)).reshape(TOKENS, N),
        eps=np.broadcast_to(a["eps"].reshape(1, 1), (P, 1)),
        w1=a["w1"],
        b1=np.broadcast_to(np.concatenate([a["b1"], a["b2"]])[None], (3, H + D)),
        rms_w=np.broadcast_to(a["rms_w"][None], (P, H)),
        w2=a["w2"],
        router_t=a["router"].T,
        ew1=up_weights(a["ew1"]), ew3=up_weights(a["ew3"]), ew2=down_weights(a["ew2"]),
    )
    arrays = {f"in_{k}": np.ascontiguousarray(v) for k, v in arrays.items()}
    nc = bacc.Bacc("TRN2", target_bir_lowering=False, num_devices=1)
    ap = {k[3:]: nc.dram_tensor(k, v.shape, F32, kind="ExternalInput").ap() for k, v in arrays.items()}
    out = nc.dram_tensor("out", (TOKENS, D), F32, kind="ExternalOutput").ap()
    graph_moe_kernel(nc, ap["x"], ap["adj_t"], ap["eps"], ap["w1"], ap["b1"], ap["rms_w"], ap["w2"], None,
                     ap["router_t"], ap["ew1"], ap["ew3"], ap["ew2"], out)
    r = run_bass_kernel_spmd(nc, [arrays], core_ids=[0])
    return r.results[0]["out"].reshape(GRAPHS, N, D)
```

```python
from contextlib import ExitStack

import concourse.bass as bass
from concourse import mybir

F32 = mybir.dt.float32
F32R = mybir.dt.float32r
BF16 = mybir.dt.bfloat16
I32 = mybir.dt.int32
U32 = mybir.dt.uint32
ALU = mybir.AluOpType
ACT = mybir.ActivationFunctionType
AX = mybir.AxisListType

P = 128
D = 128
N = 256
GRAPHS = 32
TOKENS = GRAPHS * N
TT = N // P
TILES = TOKENS // P
H = 512
HC = H // P
E = 8
EH = 341
EHP = EH + 1
CHUNKS = 3
HK = EHP // CHUNKS
TOP = 2
ROW = D + 2
ST = 2
S = ST * P
CAP = TOKENS + S
REGION_TILES = TOKENS // S
PADS = 2 * E - 1
SLOT_TILES = TOKENS * TOP // S + E - 1
LN_EPS, RMS_EPS, GATE_EPS = 1e-5, 1e-6, 1e-9
UNROLL = 4


class Step:

    def __init__(self, k, off):
        self.k, self.off = k, off

    @property
    def n(self):
        return self.k * UNROLL + self.off

    def ring(self, r):
        return self.off % r

    def turn(self, r):
        return self.k * (UNROLL // r) + self.off // r

    def plus(self, d):
        return Step(self.k, self.off + d)

    def within(self, count):
        return not isinstance(self.k, int) or 0 <= self.k * UNROLL + self.off < count


def positive(value):
    return not isinstance(value, int) or value > 0


def run_steps(eng, first, steady, bodies, last, step):
    for j in range(first, steady):
        step(Step(0, j))
    with eng.Fori(0, bodies) as k:
        for q in range(UNROLL):
            step(Step(k, steady + q))
    for j in range(steady + UNROLL * bodies, last + 1):
        step(Step(0, j))


def graph_moe_kernel(nc, x, adj_t, eps, w1, biases, rms_w, w2, router_t, ew13, ew2, out):
    ctx = ExitStack()
    with ctx:
        def sb(name, shape, dt=F32):
            return ctx.enter_context(nc.sbuf_tensor(name, shape, dt))

        def bank(name, shape, dt=F32):
            return ctx.enter_context(nc.psum_tensor(name, shape, dt))

        def sem(name):
            return ctx.enter_context(nc.semaphore(name))

        expert_rows = nc.dram_tensor("expert_rows", (E * CAP + (E - 1) * S, ROW), F32, kind="Internal").ap()
        results = nc.dram_tensor("results", (TOP * TOKENS + PADS * S, D), F32, kind="Internal").ap()

        ident = sb("ident", [P, P])
        eps_ident = sb("eps_ident", [P, P])
        eps_col = sb("eps_col", [P, 1])
        before = sb("before", [P, P], BF16)
        ones = sb("ones", [P, P], BF16)
        minus_half = sb("minus_half", [P, TT])
        expert_no = sb("expert_no", [P, E])
        region = sb("region", [P, E])
        token_no = sb("token_no", [P, TILES], I32)
        w1_sb = sb("w1_sb", [P, H])
        w1_hi = sb("w1_hi", [P, H], F32R)
        w1_lo = sb("w1_lo", [P, H], F32R)
        rms_w_sb = sb("rms_w_sb", [P, H])
        w2_sb = sb("w2_sb", [P, HC, D])
        router_sb = sb("router_sb", [P, E])
        BIAS = H + D
        bias3 = sb("bias3", [3, BIAS])
        bias_rest = sb("bias_rest", [3, 2, BIAS])
        bias_part = sb("bias_part", [3, 3, BIAS], BF16)
        bias_cut = sb("bias_cut", [3, BIAS], BF16)
        bias_sum = sb("bias_sum", [3, 2, BIAS], BF16)
        tokens = sb("tokens", [P, TILES, D])
        adj = sb("adj", [P, 2, TT, N])
        stats1 = sb("stats1", [P, 2, TT, 6])
        mean_var1 = sb("mean_var1", [P, 2, TT, 2])
        var1 = sb("var1", [P, 2, TT])
        rstd1 = sb("rstd1", [P, 2, TT])
        normed = sb("normed", [P, 2, TT, D])
        agg_hi = sb("agg_hi", [P, 2, N], F32R)
        agg_lo = sb("agg_lo", [P, 2, N], F32R)
        squares = sb("squares", [P, TT, H])
        mean_sq = sb("mean_sq", [P, 2, TT])
        mean_sq_eps = sb("mean_sq_eps", [P, 2, TT])
        rms = sb("rms", [P, 2, TT])
        scaled = sb("scaled", [P, 2, TT, H])
        hidden_t = sb("hidden_t", [P, 2, TT, HC, P])
        stats2 = sb("stats2", [P, 2, TT, 6])
        mean_var2 = sb("mean_var2", [P, 2, TT, 2])
        var2 = sb("var2", [P, 2, TT])
        rstd2 = sb("rstd2", [P, 2, TT])
        shift2 = sb("shift2", [P, 2, TT])
        rows = sb("rows", [P, 4, TOP, TT, ROW])
        normed2_t = sb("normed2_t", [P, 2, N])
        logits = sb("logits", [P, 2, TT, E])
        largest = sb("largest", [P, 2, TT, E])
        sorted_logits = sb("sorted_logits", [P, TILES, E])
        order = sb("order", [P, 2, TT, E], U32)
        chosen = sb("chosen", [P, 2, TOP, TT, E])
        mask = sb("mask", [P, 2, TT, E], BF16)
        taken = sb("taken", [P, TILES + 1, E], BF16)
        place = sb("place", [P, 2, TT, E])
        chosen_place = sb("chosen_place", [P, 2, TOP, TT, E])
        slot = sb("slot", [P, 4, TOP * TT], U32)
        gate_exp = sb("gate_exp", [P, TILES, E])
        gate_sum = sb("gate_sum", [P, TILES])
        gate_den = sb("gate_den", [P, 2, TILES])
        gate_inv = sb("gate_inv", [P, TILES])
        gates = sb("gates", [P, TOP, TILES])
        counts = sb("counts", [P, E])
        count_int = sb("count_int", [P, E], I32)
        tile_whole = sb("tile_whole", [P, E, REGION_TILES])
        tile_limit = sb("tile_limit", [P, REGION_TILES])
        tile_count = sb("tile_count", [P, E])
        tile_end = sb("tile_end", [P, E])
        zeros8 = sb("zeros8", [P, E])
        jump = sb("jump", [P, E])
        tile_no = sb("tile_no", [P, SLOT_TILES])
        passed = sb("passed", [P, SLOT_TILES, E])
        jumped = sb("jumped", [P, SLOT_TILES, E])
        tile_expert = sb("tile_expert", [P, SLOT_TILES])
        jumps = sb("jumps", [P, SLOT_TILES])
        tile_base = sb("tile_base", [P, SLOT_TILES])
        expert_int = sb("expert_int", [P, SLOT_TILES], I32)
        base_int = sb("base_int", [P, SLOT_TILES], I32)
        padding = sb("padding", [P, PADS, ST, ROW])
        ew13_sb = sb("ew13_sb", [P, E * 2 * EHP])
        up_hi = sb("up_hi", [P, 2, 2 * EHP], F32R)
        up_lo = sb("up_lo", [P, 2, 2 * EHP], F32R)
        ew2_sb = sb("ew2_sb", [HK, E * CHUNKS * D])
        slot_rows = sb("slot_rows", [P, 4, ST, ROW])
        rows_hi = sb("rows_hi", [P, 2, S], F32R)
        rows_lo = sb("rows_lo", [P, 2, S], F32R)
        silu1 = scaled[0:HK, :, :, :].rearrange("p r t h -> p r (t h)")[:, :, 0:CHUNKS * S]
        prod = hidden_t[0:HK, :, :, :, :].rearrange("p r t c n -> p r (t c n)")[:, :, 0:CHUNKS * S]
        dest = sb("dest", [P, 4, ST], U32)
        zero_int = sb("zero_int", [P, ST], U32)
        result = sb("result", [P, 4, ST, D])
        FG = 4
        picked = ew13_sb[:, 0:4 * TOP * FG * D].rearrange(
            "p (r k t d) -> p r k t d", r=4, k=TOP, t=FG)

        up_ps = [bank(f"up_ps{r}", [P, 3 * 512]) for r in range(2)]
        agg_ps = up_ps[0][:, 0:512]
        hid_ps = [up_ps[0][:, (1 + t) * 512:(2 + t) * 512] for t in range(TT)]
        hidt_ps = [up_ps[1][:, t * 512:(t + 1) * 512] for t in range(TT)]
        y_ps = up_ps[1][:, 2 * 512:3 * 512]
        rowt_ps = bank("rowt_ps", [P, 512])
        route_ps = bank("route_ps", [P, 512])
        h1_ps = [up_ps[r][0:HK, 0:CHUNKS * S] for r in range(2)]
        h3_ps = [up_ps[r][0:HK, CHUNKS * S:2 * CHUNKS * S] for r in range(2)]
        result_ps = route_ps[:, 0:ST * D]
        slots_ps = rowt_ps[:, 0:S]

        s_w1 = sem("w1_loaded"); s_bias = sem("bias_loaded"); s_small = sem("small_loaded"); s_w2 = sem("w2_loaded")
        s_ew13 = sem("ew13_loaded"); s_ew2 = sem("ew2_loaded")
        s_unit = [sem(f"unit_loaded{r}") for r in range(2)]
        s_mem = sem("constants_set"); s_const = sem("constants_ready")
        s_bcut = sem("bias_steps"); s_w1cut = sem("w1_split"); s_epsid = sem("eps_ident_ready")
        s_adj = sem("adj_ready"); s_st1 = sem("stats1_done"); s_mv1 = sem("mean_var1_done")
        s_var1 = sem("var1_ready"); s_rstd1 = sem("rstd1_ready"); s_normed = sem("normed_ready")
        s_agg = sem("agg_done"); s_agghi = sem("agg_hi_ready"); s_agglo = sem("agg_lo_ready")
        s_hid = sem("hidden_done"); s_sq = sem("squares_done"); s_msq = sem("mean_sq_ready")
        s_rms = sem("rms_ready"); s_scaled = sem("scaled_ready"); s_hidt = sem("hidden_transposed")
        s_silu = sem("silu_ready"); s_y = sem("y_done"); s_x2 = sem("tokens_updated")
        s_st2 = sem("stats2_done"); s_mv2 = sem("mean_var2_done"); s_var2 = sem("var2_ready")
        s_rstd2 = sem("rstd2_ready"); s_shift2 = sem("shift2_ready"); s_row0 = sem("first_rows_ready")
        s_row1 = sem("rows_ready"); s_rowt = sem("rows_transposed"); s_rowtc = sem("normed2_t_ready")
        s_logit = sem("logits_done"); s_route = sem("routing_steps"); s_mask = sem("mask_ready")
        s_rank = sem("rank_done"); s_place = sem("place_read"); s_slot = sem("slot_ready")
        s_sent = [sem(f"rows_sent{r}") for r in range(4)]
        s_cnt = sem("counts_done"); s_tab = sem("table_steps"); s_cplace = sem("chosen_place_ready")
        s_pad = sem("padding_ready"); s_padded = sem("padding_written"); s_cntint = sem("count_int_ready")
        s_gate = sem("gate_steps"); s_gexp = sem("gate_exp_ready")
        s_uphi = sem("up_hi_ready"); s_uplo = sem("up_lo_ready")
        s_slotrow = [sem(f"slot_rows_loaded{r}") for r in range(4)]
        s_xt = sem("slot_rows_transposed"); s_xhi = sem("rows_hi_ready"); s_xlo = sem("rows_lo_ready")
        s_h1 = sem("h1_done"); s_h3 = sem("h3_done"); s_silu1 = sem("silu1_ready"); s_dest = sem("dest_ready")
        s_prod = sem("prod_ready"); s_base = sem("bases_ready"); s_expert = sem("tile_experts_ready")
        s_yy = sem("expert_y_done"); s_res = sem("result_ready")
        s_resout = [sem(f"results_sent{r}") for r in range(4)]
        s_picked = [sem(f"picked_loaded{r}") for r in range(4)]
        s_sum1 = sem("first_choice_added"); s_sum2 = sem("second_choice_added")
        s_out = [sem(f"out_written{r}") for r in range(4)]

        G = dict(first=-3, steady=5, bodies=(GRAPHS - 3 - 5) // UNROLL, last=GRAPHS + 3)
        X = dict(first=-1, steady=7, bodies=(SLOT_TILES - 1 - 7) // UNROLL, last=SLOT_TILES + 1)

        def run_expert_steps(eng, kind, ahead, step):
            def some(i, count):
                low = max(0, -ahead - i.off) if isinstance(i.k, int) else 0
                high = min(count, SLOT_TILES - ahead - i.off) if isinstance(i.k, int) else count
                experts = [None] * count
                if low < high:
                    _, experts[low:high] = nc.values_load_multi_w_load_instructions(
                        expert_int[0:1, bass.ds(i.plus(low + ahead).n, high - low)], engines=[kind], min_val=0,
                        max_val=E - 1, skip_runtime_bounds_check_because="sums of E - 1 comparisons")
                for q in range(count):
                    step(i.plus(q), experts[q])

            for j in range(X["first"], X["steady"], UNROLL):
                some(Step(0, j), UNROLL)
            with eng.Fori(0, X["bodies"]) as k:
                some(Step(k, X["steady"]), UNROLL)
            for j in range(X["steady"] + UNROLL * X["bodies"], X["last"] + 1, UNROLL):
                some(Step(0, j), min(UNROLL, X["last"] + 1 - j))

        block = ctx.enter_context(nc.Block())

        @block.sync
        def _(sp):
            sp.dma_start(bias3[:, :], biases).then_inc(s_bias, 16)
            sp.dma_start(w1_sb[:, :], w1).then_inc(s_w1, 16)

            def load_unit(u):
                if positive(u.plus(-1).n):
                    sp.wait_ge(s_agg, u.plus(-1).n)
                sp.dma_start(tokens[:, bass.ds(u.n * TT, TT), :],
                             x.rearrange("(t p) d -> p t d", p=P)[:, bass.ds(u.n * TT, TT), :]
                             ).then_inc(s_unit[u.ring(2)], 16)
                sp.dma_start(adj[:, u.ring(2), :, :],
                             adj_t.rearrange("(b c p) n -> p b c n", p=P, c=TT)[:, bass.ds(u.n, 1), :, :]
                             .rearrange("p b c n -> p (b c) n")
                             ).then_inc(s_unit[u.ring(2)], 16)

            for u in range(4):
                load_unit(Step(0, u))
                if u == 0:
                    sp.dma_start(w2_sb[:, :, :], w2.rearrange("(c p) d -> p c d", p=P)).then_inc(s_w2, 16)
                if u == 3:
                    sp.dma_start(ew13_sb[:, :], ew13).then_inc(s_ew13, 16)
                    sp.dma_start(ew2_sb[:, :], ew2).then_inc(s_ew2, 16)
            with sp.Fori(1, GRAPHS // UNROLL) as k:
                for q in range(UNROLL):
                    load_unit(Step(k, q))

            sp.wait_ge(s_pad, 1)
            sp.dma_start(expert_rows[E * CAP:E * CAP + (E - 1) * S, :].rearrange("(b p h) r -> p b h r", p=P, h=ST),
                         padding[:, E:PADS, :, :]).then_inc(s_padded, 16)
            sp.wait_ge(s_cntint, 1)
            _, found = nc.values_load_multi_w_load_instructions(
                count_int[0:1, :], engines=[mybir.EngineType.SP], min_val=0, max_val=TOKENS,
                skip_runtime_bounds_check_because="an expert has at most one row of every token")
            for e in range(E):
                sp.dma_start(expert_rows[bass.ds(found[e] + e * CAP, S), :].rearrange("(p h) r -> p h r", h=ST),
                             padding[:, e, :, :]).then_inc(s_padded, 16)
            sp.wait_ge(s_padded, 16 * (E + 1))
            for r in range(4):
                sp.wait_ge(s_sent[r], 16 * TOP * TT * (GRAPHS // 4))
            sp.wait_ge(s_base, 1)

            def bases_of(i, count):
                _, bases = nc.values_load_multi_w_load_instructions(
                    base_int[0:1, bass.ds(i.n, count)], engines=[mybir.EngineType.SP], min_val=0,
                    max_val=E * CAP + (E - 2) * S,
                    skip_runtime_bounds_check_because="the list holds SLOT_TILES tiles, each within its region")
                return bases

            def load_slots(i, base):
                if positive(i.plus(-3).n):
                    sp.wait_ge(s_xt, i.plus(-3).n)
                    sp.wait_ge(s_dest, i.plus(-3).n)
                sp.dma_start(slot_rows[:, i.ring(4), :, :],
                             expert_rows[bass.ds(base, S), :].rearrange("(p h) r -> p h r", h=ST)
                             ).then_inc(s_slotrow[i.ring(4)], 16)

            def load_some(i, count):
                for q, base in enumerate(bases_of(i, count)):
                    load_slots(i.plus(q), base)

            load_some(Step(0, 0), UNROLL)
            with sp.Fori(1, SLOT_TILES // UNROLL) as k:
                load_some(Step(k, 0), UNROLL)
            left = SLOT_TILES % UNROLL
            load_some(Step(0, SLOT_TILES - left), left)

            for r in range(4):
                sp.wait_ge(s_resout[r], 16 * ST * ((SLOT_TILES + 3 - r) // 4))
            STEPS = TILES // FG
            picks = results[0:TOP * TOKENS, :].rearrange("(k t p) d -> p k t d", p=P, k=TOP)

            def load_picked(g):
                if positive(g.plus(-3).n):
                    sp.wait_ge(s_sum2, g.plus(-3).n)
                for c in range(TOP):
                    sp.dma_start(picked[:, g.ring(4), c, :, :],
                                 picks[:, c, bass.ds(g.n * FG, FG), :]).then_inc(s_picked[g.ring(4)], 16)

            for q in range(UNROLL):
                load_picked(Step(0, q))
            with sp.Fori(1, STEPS // UNROLL) as k:
                for q in range(UNROLL):
                    load_picked(Step(k, q))
            for r in range(4):
                sp.wait_ge(s_out[r], 16 * (STEPS // 4))

        @block.gpsimd
        def _(pool):
            pool.memset(ident[:, :], 0.0).then_inc(s_mem, 1)
            pool.memset(before[:, :], 1.0).then_inc(s_mem, 1)
            pool.memset(ones[:, :], 1.0).then_inc(s_const, 1)
            pool.memset(minus_half[:, :], -0.5).then_inc(s_const, 1)
            pool.wait_ge(s_mem, 2)
            pool.affine_select(out=ident[:, :], in_=ident[:, :], compare_op=ALU.not_equal, fill=1.0,
                               base=0, pattern=[[-1, P]], channel_multiplier=1).then_inc(s_const, 1)
            pool.affine_select(out=before[:, :], in_=before[:, :], compare_op=ALU.is_gt, fill=0.0,
                               base=0, pattern=[[1, P]], channel_multiplier=-1).then_inc(s_const, 1)
            pool.iota(expert_no[:, :], pattern=[[1, E]], base=0, channel_multiplier=0,
                      allow_small_or_imprecise_dtypes=True).then_inc(s_const, 1)
            pool.iota(token_no[:, :], pattern=[[P, TILES]], base=0, channel_multiplier=1).then_inc(s_const, 1)
            pool.iota(region[:, :], pattern=[[CAP, E]], base=0, channel_multiplier=0,
                      allow_small_or_imprecise_dtypes=True).then_inc(s_const, 1)
            pool.iota(tile_no[:, :], pattern=[[1, SLOT_TILES]], base=0, channel_multiplier=0,
                      allow_small_or_imprecise_dtypes=True).then_inc(s_const, 1)
            pool.iota(tile_limit[:, :], pattern=[[S, REGION_TILES]], base=0, channel_multiplier=0,
                      allow_small_or_imprecise_dtypes=True).then_inc(s_const, 1)
            pool.memset(taken[:, 0, :], 0.0).then_inc(s_const, 1)
            pool.memset(zeros8[:, :], 0.0)
            pool.memset(zero_int[:, :], 0).then_inc(s_const, 1)
            pool.memset(rows[:, :, :, :, D + 1:ROW], 0.0).then_inc(s_const, 1)
            pool.memset(padding[:, :, :, :], 0.0).then_inc(s_mem, 1)
            pool.wait_ge(s_mem, 3)
            pool.iota(padding[:, :, :, D].bitcast(I32), pattern=[[S, PADS], [P, ST]], base=TOP * TOKENS,
                      channel_multiplier=1).then_inc(s_pad, 1)

            def rstd1_of(u):
                pool.wait_ge(s_var1, u.plus(1).n)
                r = u.ring(2)
                if positive(u.plus(-1).n):
                    pool.wait_ge(s_normed, u.plus(-1).n)
                pool.tensor_tensor(rstd1[:, r, :], var1[:, r, :], minus_half[:, :], ALU.pow).then_inc(s_rstd1, 1)

            def rms_of(u):
                pool.wait_ge(s_msq, u.plus(1).n)
                r = u.ring(2)
                if positive(u.plus(-1).n):
                    pool.wait_ge(s_scaled, u.plus(-1).n * TT)
                pool.tensor_tensor(rms[:, r, :], mean_sq_eps[:, r, :], minus_half[:, :], ALU.pow).then_inc(s_rms, 1)

            def rstd2_of(u):
                sent = u.plus(-3)
                if sent.within(GRAPHS):
                    pool.wait_ge(s_slot, sent.plus(1).n)
                    pool.wait_ge(s_row1, sent.plus(1).n)
                if not u.within(GRAPHS):
                    return
                pool.wait_ge(s_var2, u.plus(1).n)
                r = u.ring(2)
                if positive(u.plus(-1).n):
                    pool.wait_ge(s_row0, u.plus(-1).n)
                pool.tensor_tensor(rstd2[:, r, :], var2[:, r, :], minus_half[:, :], ALU.pow).then_inc(s_rstd2, 1)

            def send(u, c):
                r = u.ring(4)
                for t in range(TT):
                    pool.indirect_dma_start(
                        out=expert_rows, out_offset=bass.IndirectOffsetOnAxis(
                            ap=slot[:, r, c * TT + t:c * TT + t + 1], axis=0),
                        in_=rows[:, r, c, t, :], in_offset=None).then_inc(s_sent[r], 16)

            def step(j):
                rstd2_of(j.plus(-1))
                if j.plus(-4).within(GRAPHS):
                    send(j.plus(-4), 0)
                if j.plus(3).within(GRAPHS):
                    rstd1_of(j.plus(3))
                if j.plus(1).within(GRAPHS):
                    rms_of(j.plus(1))
                if j.plus(-4).within(GRAPHS):
                    send(j.plus(-4), 1)

            pool.wait_ge(s_const, 4)
            run_steps(pool, G["first"], G["steady"] + 1, G["bodies"] - 1, G["last"], step)

            def destinations(i):
                q = i.ring(4)
                pool.wait_ge(s_slotrow[q], i.turn(4) * 16 + 16)
                if positive(i.turn(4)):
                    pool.wait_ge(s_resout[q], i.turn(4) * (16 * ST))
                pool.tensor_tensor(dest[:, q, :], slot_rows[:, q, :, D].bitcast(U32), zero_int[:, :],
                                   ALU.add).then_inc(s_dest, 1)

            def send_result(i, ahead):
                pool.wait_ge(s_res, i.plus(1).n)
                pool.wait_ge(s_dest, i.plus(1).n)
                if ahead.within(SLOT_TILES):
                    destinations(ahead)
                r = i.ring(4)
                for h in range(ST):
                    pool.indirect_dma_start(
                        out=results, out_offset=bass.IndirectOffsetOnAxis(ap=dest[:, r, h:h + 1], axis=0),
                        in_=result[:, r, h, :], in_offset=None).then_inc(s_resout[r], 16)

            def expert_step(i):
                if i.within(SLOT_TILES):
                    send_result(i, i.plus(2))
                else:
                    destinations(i.plus(2))

            run_steps(pool, -2, 4, (SLOT_TILES - 2 - 4) // UNROLL, SLOT_TILES - 1, expert_step)

        @block.scalar
        def _(act):
            act.dma_start(rms_w_sb[:, :], rms_w).then_inc(s_small, 16)
            act.dma_start(router_sb[:, :], router_t).then_inc(s_small, 16)
            act.dma_start(eps_col[:, :], eps).then_inc(s_small, 16)

            def agg_high(u):
                r = u.ring(2)
                act.wait_ge(s_agg, u.plus(1).n)
                if positive(u.plus(-1).n):
                    act.wait_ge(s_hid, u.plus(-1).n * TT)
                act.activation(agg_hi[:, r, :], agg_ps[:, 0:N], ACT.Copy).then_inc(s_agghi, 1)

            def silu_of(u):
                r = u.ring(2)
                for t in range(TT):
                    act.wait_ge(s_hidt, u.n * TT + t + 1)
                    if t == 0 and positive(u.plus(-1).n):
                        act.wait_ge(s_y, u.plus(-1).n)
                    act.activation(hidden_t[:, r, t, :, :].rearrange("p c n -> p (c n)"), hidt_ps[t][:, :],
                                   ACT.Silu).then_inc(s_silu, 1)

            def normed_rows(u):
                r = u.ring(2)
                act.wait_ge(s_shift2, u.plus(1).n)
                if positive(u.turn(4)):
                    act.wait_ge(s_sent[u.ring(4)], u.turn(4) * (16 * TOP * TT))
                for t in range(TT):
                    ins = act.activation(rows[:, u.ring(4), 0, t, 0:D], tokens[:, u.n * TT + t, :], ACT.Identity,
                                         bias=shift2[:, r, t:t + 1], scale=rstd2[:, r, t:t + 1])
                ins.then_inc(s_row0, 1)

            def squares_of(u):
                r = u.ring(2)
                if positive(u.plus(-1).n):
                    act.wait_ge(s_msq, u.plus(-1).n)
                for t in range(TT):
                    act.wait_ge(s_hid, u.n * TT + t + 1)
                    if positive(u.n):
                        act.wait_ge(s_sq, u.n * TT + t - 1)
                    act.activation(squares[:, t, :], hid_ps[t][:, :], ACT.Square, scale=float(H) ** -0.5,
                                   accum_out=mean_sq[:, r, t:t + 1]).then_inc(s_sq, 1)

            def rows_t(u):
                r = u.ring(2)
                act.wait_ge(s_rowt, u.plus(1).n)
                if positive(u.plus(-1).n):
                    act.wait_ge(s_logit, u.plus(-1).n)
                act.activation(normed2_t[:, r, :], rowt_ps[:, 0:N], ACT.Copy).then_inc(s_rowtc, 1)

            def step(j):
                if j.plus(2).within(GRAPHS):
                    agg_high(j.plus(2))
                if j.within(GRAPHS):
                    silu_of(j)
                if j.plus(-1).within(GRAPHS):
                    normed_rows(j.plus(-1))
                if j.plus(1).within(GRAPHS):
                    squares_of(j.plus(1))
                if j.plus(-2).within(GRAPHS):
                    rows_t(j.plus(-2))

            act.wait_ge(s_const, 12)
            run_steps(act, G["first"], G["steady"], G["bodies"], G["last"], step)

            act.wait_ge(s_gate, 1)
            act.activation(gate_exp[:, :, :], gate_exp[:, :, :], ACT.Exp).then_inc(s_gexp, 1)

            act.wait_ge(s_ew13, 16)
            act.wait_ge(s_expert, 1)

            def weights_high(i, expert):
                if positive(i.plus(-1).n):
                    act.wait_ge(s_h3, i.plus(-1).n)
                act.activation(up_hi[:, i.ring(2), :], ew13_sb[:, bass.ds(expert * (2 * EHP), 2 * EHP)],
                               ACT.Copy).then_inc(s_uphi, 1)

            def silu_h1(i):
                r = i.ring(2)
                act.wait_ge(s_h1, i.plus(1).n)
                act.activation(silu1[:, r, :], h1_ps[r], ACT.Silu).then_inc(s_silu1, 1)

            def rows_high(i):
                act.wait_ge(s_xt, i.plus(1).n)
                act.activation(rows_hi[:, i.ring(2), :], slots_ps, ACT.Copy).then_inc(s_xhi, 1)

            def expert_step(i, next_expert):
                if i.plus(1).within(SLOT_TILES):
                    weights_high(i.plus(1), next_expert)
                if i.within(SLOT_TILES):
                    silu_h1(i)
                if i.plus(1).within(SLOT_TILES):
                    rows_high(i.plus(1))

            run_expert_steps(act, mybir.EngineType.Activation, 1, expert_step)

            out_t = out.rearrange("(t p) d -> p t d", p=P)

            def store(g):
                act.wait_ge(s_sum2, g.plus(1).n)
                act.dma_start(out_t[:, bass.ds(g.n * FG, FG), :],
                              tokens[:, bass.ds(g.n * FG, FG), :]).then_inc(s_out[g.ring(4)], 16)

            with act.Fori(0, TILES // FG // UNROLL) as k:
                for q in range(UNROLL):
                    store(Step(k, q))

        @block.tensor
        def _(pe):
            def sum_neighbours(u):
                r = u.ring(2)
                pe.wait_ge(s_normed, u.plus(1).n)
                pe.wait_ge(s_adj, u.plus(1).n)
                if positive(u.n):
                    pe.wait_ge(s_agglo, u.n)
                for c in range(TT):
                    ins = pe.matmul(agg_ps[:, 0:N], normed[:, r, c, :], adj[:, r, c, :], start=(c == 0), stop=(c == TT - 1))
                ins.then_inc(s_agg, 1)

            def transpose_hidden(u):
                for t in range(TT):
                    pe.wait_ge(s_scaled, u.n * TT + t + 1)
                    if positive(u.n):
                        pe.wait_ge(s_silu, u.n * TT + t - 1)
                    for c in range(HC):
                        ins = pe.transpose(hidt_ps[t][:, c * P:(c + 1) * P],
                                           scaled[:, u.ring(2), t, c * P:(c + 1) * P], ident[:, :])
                    ins.then_inc(s_hidt, 1)

            def first_product(u):
                r = u.ring(2)
                pe.wait_ge(s_agglo, u.plus(1).n)
                for t in range(TT):
                    if positive(u.n):
                        pe.wait_ge(s_scaled, u.n * TT + t - 1)
                    hi, lo = agg_hi[:, r, t * P:(t + 1) * P], agg_lo[:, r, t * P:(t + 1) * P]
                    pe.matmul(hid_ps[t][:, :], ones[0:3, :], bias_cut[:, 0:H], start=True, stop=False)
                    pe.matmul(hid_ps[t][:, :], lo, w1_hi[:, :], start=False, stop=False)
                    pe.matmul(hid_ps[t][:, :], hi, w1_lo[:, :], start=False, stop=False)
                    pe.matmul(hid_ps[t][:, :], hi, w1_hi[:, :], start=False, stop=True).then_inc(s_hid, 1)

            def second_product(u):
                if positive(u.n):
                    pe.wait_ge(s_x2, u.n)
                for t in range(TT):
                    pe.wait_ge(s_silu, u.n * TT + t + 1)
                    pe.matmul(y_ps[:, t * D:(t + 1) * D], ones[0:3, :], bias_cut[:, H:H + D], start=True, stop=False)
                    for c in range(HC):
                        ins = pe.matmul(y_ps[:, t * D:(t + 1) * D], hidden_t[:, u.ring(2), t, c, :], w2_sb[:, c, :],
                                        start=False, stop=(c == HC - 1))
                ins.then_inc(s_y, 1)

            def transpose_rows(u):
                pe.wait_ge(s_row0, u.plus(1).n)
                if positive(u.n):
                    pe.wait_ge(s_rowtc, u.n)
                for t in range(TT):
                    ins = pe.transpose(rowt_ps[:, t * P:(t + 1) * P], rows[:, u.ring(4), 0, t, 0:D], ident[:, :])
                ins.then_inc(s_rowt, 1)

            def router(u):
                pe.wait_ge(s_rowtc, u.plus(1).n)
                if positive(u.n):
                    pe.wait_ge(s_place, u.n)
                for t in range(TT):
                    ins = pe.matmul(route_ps[:, t * E:(t + 1) * E], normed2_t[:, u.ring(2), t * P:(t + 1) * P],
                                    router_sb[:, :], start=True, stop=True)
                ins.then_inc(s_logit, 1)

            def rank(u):
                pe.wait_ge(s_mask, u.plus(1).n)
                for t in range(TT):
                    part = route_ps[:, 64 + t * E:64 + (t + 1) * E]
                    pe.matmul(part, before[:, :], mask[:, u.ring(2), t, :], start=True, stop=False)
                    ins = pe.matmul(part, ones[:, :], taken[:, u.n * TT + t, :], start=False, stop=True)
                ins.then_inc(s_rank, 1)

            def step(j):
                if j.plus(2).within(GRAPHS):
                    sum_neighbours(j.plus(2))
                if j.within(GRAPHS):
                    transpose_hidden(j)
                if j.plus(-3).within(GRAPHS):
                    rank(j.plus(-3))
                if j.plus(1).within(GRAPHS):
                    first_product(j.plus(1))
                if j.plus(-2).within(GRAPHS):
                    transpose_rows(j.plus(-2))
                if j.within(GRAPHS):
                    second_product(j)
                if j.plus(-2).within(GRAPHS):
                    router(j.plus(-2))

            pe.wait_ge(s_const, 12)
            pe.wait_ge(s_small, 48)
            pe.wait_ge(s_w2, 16)
            pe.wait_ge(s_w1cut, 2)
            pe.wait_ge(s_bcut, 9)
            run_steps(pe, G["first"], G["steady"], G["bodies"], G["last"], step)

            pe.wait_ge(s_place, GRAPHS)
            pe.matmul(route_ps[:, 0:E], ones[:, :], taken[:, TILES, :], start=True, stop=True).then_inc(s_cnt, 1)

            pe.wait_ge(s_ew2, 16)
            pe.wait_ge(s_tab, 1)
            pe.wait_ge(s_expert, 1)

            def transpose_slots(i):
                pe.wait_ge(s_slotrow[i.ring(4)], i.turn(4) * 16 + 16)
                for h in range(ST):
                    ins = pe.transpose(slots_ps[:, h * P:(h + 1) * P], slot_rows[:, i.ring(4), h, 0:D],
                                       ident[:, :])
                ins.then_inc(s_xt, 1)

            def up(i):
                r = i.ring(2)
                pe.wait_ge(s_xlo, i.plus(1).n)
                for k, ps in ((0, h1_ps[r]), (1, h3_ps[r])):
                    for c in range(CHUNKS):
                        part = ps[:, c * S:(c + 1) * S]
                        at = slice(k * EHP + c * HK, k * EHP + (c + 1) * HK)
                        pe.matmul(part, up_hi[:, r, at], rows_lo[:, r, :], start=True, stop=False)
                        pe.matmul(part, up_lo[:, r, at], rows_hi[:, r, :], start=False, stop=False)
                        ins = pe.matmul(part, up_hi[:, r, at], rows_hi[:, r, :], start=False, stop=True)
                        if k == 1 and c == 0:
                            ins.then_inc(s_h1, 1)
                ins.then_inc(s_h3, 1)

            def down(i, expert):
                r = i.ring(2)
                pe.wait_ge(s_prod, i.plus(1).n)
                if positive(i.n):
                    pe.wait_ge(s_res, i.n)
                for h in range(ST):
                    for c in range(CHUNKS):
                        ins = pe.matmul(result_ps[:, h * D:(h + 1) * D],
                                        prod[:, r, c * S + h * P:c * S + (h + 1) * P],
                                        ew2_sb[:, bass.ds((expert * CHUNKS + c) * D, D)],
                                        start=(c == 0), stop=(c == CHUNKS - 1))
                ins.then_inc(s_yy, 1)

            def expert_step(i, expert_before):
                if i.within(SLOT_TILES):
                    up(i)
                if i.plus(1).within(SLOT_TILES):
                    transpose_slots(i.plus(1))
                if i.plus(-1).within(SLOT_TILES):
                    down(i.plus(-1), expert_before)

            run_expert_steps(pe, mybir.EngineType.PE, -1, expert_step)

        @block.vector
        def _(dve):
            dve.wait_ge(s_w1, 16)
            dve.tensor_copy(w1_hi[:, :], w1_sb[:, :]).then_inc(s_w1cut, 1)
            dve.wait_ge(s_w1cut, 1)
            dve.tensor_tensor(w1_lo[:, :], w1_sb[:, :], w1_hi[:, :].bitcast(F32), ALU.subtract).then_inc(s_w1cut, 1)
            dve.wait_ge(s_bias, 16)
            dve.tensor_copy(bias_part[:, 0, :], bias3[:, :]).then_inc(s_bcut, 1)
            dve.wait_ge(s_bcut, 1)
            dve.tensor_tensor(bias_rest[:, 0, :], bias3[:, :], bias_part[:, 0, :], ALU.subtract).then_inc(s_bcut, 1)
            dve.wait_ge(s_bcut, 2)
            dve.tensor_copy(bias_part[:, 1, :], bias_rest[:, 0, :]).then_inc(s_bcut, 1)
            dve.wait_ge(s_bcut, 3)
            dve.tensor_tensor(bias_rest[:, 1, :], bias_rest[:, 0, :], bias_part[:, 1, :], ALU.subtract).then_inc(s_bcut, 1)
            dve.wait_ge(s_bcut, 4)
            dve.tensor_copy(bias_part[:, 2, :], bias_rest[:, 1, :]).then_inc(s_bcut, 1)
            dve.wait_ge(s_const, 12)
            dve.wait_ge(s_bcut, 5)
            dve.tensor_scalar(bias_sum[:, 0, :], bias_part[:, 0, :], ident[0:3, 0:1], None, ALU.mult).then_inc(s_bcut, 1)
            dve.wait_ge(s_bcut, 6)
            dve.scalar_tensor_tensor(out=bias_sum[:, 1, :], in0=bias_part[:, 1, :], scalar=ident[0:3, 1:2],
                                     in1=bias_sum[:, 0, :], op0=ALU.mult, op1=ALU.add).then_inc(s_bcut, 1)
            dve.wait_ge(s_bcut, 7)
            dve.scalar_tensor_tensor(out=bias_cut[:, :], in0=bias_part[:, 2, :], scalar=ident[0:3, 2:3],
                                     in1=bias_sum[:, 1, :], op0=ALU.mult, op1=ALU.add).then_inc(s_bcut, 1)
            dve.wait_ge(s_small, 48)
            dve.tensor_scalar(eps_ident[:, :], ident[:, :], eps_col[:, 0:1], None, ALU.mult).then_inc(s_bcut, 1)
            dve.wait_ge(s_bcut, 9)

            def normalise1(u):
                r = u.ring(2)
                dve.wait_ge(s_rstd1, u.plus(1).n)
                if positive(u.plus(-1).n):
                    dve.wait_ge(s_agg, u.plus(-1).n)
                for t in range(TT):
                    ins = dve.tensor_scalar(normed[:, r, t, :], tokens[:, u.n * TT + t, :], mean_var1[:, r, t, 0:1],
                                            rstd1[:, r, t:t + 1], ALU.subtract, ALU.mult)
                ins.then_inc(s_normed, 1)

            def agg_low(u):
                r = u.ring(2)
                dve.wait_ge(s_agghi, u.plus(1).n)
                if positive(u.plus(-1).n):
                    dve.wait_ge(s_hid, u.plus(-1).n * TT)
                dve.tensor_tensor(agg_lo[:, r, :], agg_ps[:, 0:N], agg_hi[:, r, :].bitcast(F32),
                                  ALU.subtract).then_inc(s_agglo, 1)

            def mean_square(u):
                r = u.ring(2)
                dve.wait_ge(s_sq, u.n * TT + TT)
                dve.tensor_scalar(mean_sq_eps[:, r, :], mean_sq[:, r, :], RMS_EPS, None, ALU.add).then_inc(s_msq, 1)

            def scale_hidden(u):
                r = u.ring(2)
                dve.wait_ge(s_rms, u.plus(1).n)
                if positive(u.plus(-1).n):
                    dve.wait_ge(s_hidt, u.plus(-1).n * TT)
                for t in range(TT):
                    dve.scalar_tensor_tensor(out=scaled[:, r, t, :], in0=hid_ps[t][:, :], scalar=rms[:, r, t:t + 1],
                                             in1=rms_w_sb[:, :], op0=ALU.mult, op1=ALU.mult).then_inc(s_scaled, 1)

            def shift_of(u):
                r = u.ring(2)
                dve.wait_ge(s_rstd2, u.plus(1).n)
                if positive(u.plus(-1).n):
                    dve.wait_ge(s_row0, u.plus(-1).n)
                dve.scalar_tensor_tensor(out=shift2[:, r, :], in0=mean_var2[:, r, :, 0], scalar=-1.0,
                                         in1=rstd2[:, r, :], op0=ALU.mult, op1=ALU.mult).then_inc(s_shift2, 1)

            def finish_rows(u):
                q = u.ring(4)
                dve.wait_ge(s_row0, u.plus(1).n)
                if positive(u.turn(4)):
                    dve.wait_ge(s_sent[q], u.turn(4) * (16 * TOP * TT))
                dve.tensor_copy(rows[:, q, 1, :, 0:D], rows[:, q, 0, :, 0:D])
                for c in range(TOP):
                    ins = dve.tensor_scalar(rows[:, q, c, :, D].bitcast(I32), token_no[:, bass.ds(u.n * TT, TT)],
                                            float(c * TOKENS), None, ALU.add)
                ins.then_inc(s_row1, 1)

            def statistics(fresh, ended, routed):
                f, d, r = fresh.ring(2), ended.ring(2), routed.ring(2)
                is_fresh, is_ended, is_routed = (u.within(GRAPHS) for u in (fresh, ended, routed))
                if is_ended:
                    dve.wait_ge(s_y, ended.plus(1).n)
                    mine = tokens[:, bass.ds(ended.n * TT, TT), :]
                    dve.tensor_tensor(mine, y_ps[:, 0:TT * D].rearrange("p (t d) -> p t d", t=TT), mine,
                                      ALU.add).then_inc(s_x2, 1)
                if is_routed:
                    dve.wait_ge(s_logit, routed.plus(1).n)
                    dve.tensor_copy(logits[:, r, :, :].rearrange("p t e -> p (t e)"),
                                    route_ps[:, 0:TT * E]).then_inc(s_route, 1)
                if is_ended:
                    dve.wait_ge(s_x2, ended.plus(1).n)
                if is_routed:
                    dve.wait_ge(s_route, routed.n * 6 + 1)
                if is_fresh:
                    dve.wait_ge(s_unit[f], fresh.turn(2) * 32 + 32)
                    for c in range(TT):
                        part = adj[:, f, c, c * P:(c + 1) * P]
                        ins = dve.tensor_tensor(part, part, eps_ident[:, :], ALU.add)
                    ins.then_inc(s_adj, 1)
                    for t in range(TT):
                        ins = dve.bn_stats(stats1[:, f, t, :], tokens[:, fresh.n * TT + t, :])
                    ins.then_inc(s_st1, 1)
                if is_ended:
                    for t in range(TT):
                        ins = dve.bn_stats(stats2[:, d, t, :], tokens[:, ended.n * TT + t, :])
                    ins.then_inc(s_st2, 1)
                if is_routed:
                    for t in range(TT):
                        ins = dve.max(largest[:, r, t, :], logits[:, r, t, :])
                    ins.then_inc(s_route, 1)
                if is_fresh:
                    dve.wait_ge(s_st1, fresh.plus(1).n)
                if is_ended:
                    dve.wait_ge(s_st2, ended.plus(1).n)
                if is_routed:
                    dve.wait_ge(s_route, routed.n * 6 + 2)
                    dve.tensor_copy(sorted_logits[:, bass.ds(routed.n * TT, TT), :], largest[:, r, :, :])
                if is_fresh:
                    for t in range(TT):
                        ins = dve.bn_aggr(mean_var1[:, f, t, :], stats1[:, f, t, :])
                    ins.then_inc(s_mv1, 1)
                if is_ended:
                    for t in range(TT):
                        ins = dve.bn_aggr(mean_var2[:, d, t, :], stats2[:, d, t, :])
                    ins.then_inc(s_mv2, 1)
                if is_routed:
                    for t in range(TT):
                        ins = dve.max_index(order[:, r, t, :], largest[:, r, t, :], logits[:, r, t, :])
                    ins.then_inc(s_route, 1)
                if is_ended:
                    dve.wait_ge(s_mv2, ended.plus(1).n)
                    dve.tensor_scalar(var2[:, d, :], mean_var2[:, d, :, 1], LN_EPS, None, ALU.add).then_inc(s_var2, 1)
                if is_fresh:
                    dve.wait_ge(s_mv1, fresh.plus(1).n)
                    dve.tensor_scalar(var1[:, f, :], mean_var1[:, f, :, 1], LN_EPS, None, ALU.add).then_inc(s_var1, 1)

            def choose(u):
                r = u.ring(2)
                dve.wait_ge(s_route, u.n * 6 + 3)
                for c in range(TOP):
                    ins = dve.tensor_tensor(chosen[:, r, c, :, :], expert_no[:, :].unsqueeze(1).to_broadcast([P, TT, E]),
                                            order[:, r, :, c:c + 1].to_broadcast([P, TT, E]), ALU.is_equal)
                ins.then_inc(s_route, 1)
                dve.wait_ge(s_route, u.n * 6 + 4)
                if positive(u.plus(-1).n):
                    dve.wait_ge(s_rank, u.plus(-1).n)
                dve.tensor_tensor(mask[:, r, :, :], chosen[:, r, 0, :, :], chosen[:, r, 1, :, :],
                                  ALU.add).then_inc(s_route, 1)
                dve.wait_ge(s_route, u.n * 6 + 5)
                dve.tensor_tensor(taken[:, u.n * TT + 1, :], taken[:, u.n * TT, :], mask[:, r, 0, :],
                                  ALU.add).then_inc(s_route, 1)
                dve.wait_ge(s_route, u.n * 6 + 6)
                dve.tensor_tensor(taken[:, u.n * TT + 2, :], taken[:, u.n * TT + 1, :], mask[:, r, 1, :],
                                  ALU.add).then_inc(s_mask, 1)

            def slots_of(u):
                r, q = u.ring(2), u.ring(4)
                dve.wait_ge(s_rank, u.plus(1).n)
                dve.tensor_tensor(place[:, r, :, :], route_ps[:, 64:64 + TT * E].rearrange("p (t e) -> p t e", t=TT),
                                  region[:, :].unsqueeze(1).to_broadcast([P, TT, E]), ALU.add).then_inc(s_place, 1)
                dve.wait_ge(s_place, u.plus(1).n)
                for c in range(TOP):
                    ins = dve.tensor_tensor(chosen_place[:, r, c, :, :], chosen[:, r, c, :, :], place[:, r, :, :], ALU.mult)
                ins.then_inc(s_cplace, 1)
                dve.wait_ge(s_cplace, u.plus(1).n)
                if positive(u.turn(4)):
                    dve.wait_ge(s_sent[q], u.turn(4) * (16 * TOP * TT))
                with nc.allow_low_precision(reason="whole numbers below 2**24, added in float32: exact"):
                    dve.tensor_reduce(slot[:, q, :].rearrange("p (c t) -> p c t", c=TOP),
                                      chosen_place[:, r, :, :, :], AX.X, ALU.add).then_inc(s_slot, 1)

            def step(j):
                statistics(j.plus(3), j.plus(-1), j.plus(-3))
                if j.plus(-3).within(GRAPHS):
                    choose(j.plus(-3))
                if j.plus(2).within(GRAPHS):
                    agg_low(j.plus(2))
                if j.plus(-1).within(GRAPHS):
                    shift_of(j.plus(-1))
                if j.plus(-3).within(GRAPHS):
                    slots_of(j.plus(-3))
                if j.plus(3).within(GRAPHS):
                    normalise1(j.plus(3))
                if j.plus(-1).within(GRAPHS):
                    finish_rows(j.plus(-1))
                if j.plus(1).within(GRAPHS):
                    mean_square(j.plus(1))
                    scale_hidden(j.plus(1))

            run_steps(dve, G["first"], G["steady"], G["bodies"], G["last"], step)

            dve.wait_ge(s_cnt, 1)
            dve.tensor_copy(counts[:, :], route_ps[:, 0:E]).then_inc(s_tab, 1)
            dve.wait_ge(s_tab, 1)
            dve.tensor_copy(count_int[:, :], counts[:, :]).then_inc(s_cntint, 1)
            dve.tensor_tensor(tile_whole[:, :, :], counts[:, :].unsqueeze(2).to_broadcast([P, E, REGION_TILES]),
                              tile_limit[:, :].unsqueeze(1).to_broadcast([P, E, REGION_TILES]),
                              ALU.is_gt).then_inc(s_tab, 1)
            dve.wait_ge(s_tab, 2)
            dve.tensor_reduce(tile_count[:, :], tile_whole[:, :, :], AX.X, ALU.add).then_inc(s_tab, 1)
            dve.wait_ge(s_tab, 3)
            dve.tensor_tensor_scan(tile_end[:, :], tile_count[:, :], zeros8[:, :], 0.0, ALU.add,
                                   ALU.add).then_inc(s_tab, 1)
            dve.tensor_scalar(jump[:, :], tile_count[:, :], float(-S), float(CAP), ALU.mult, ALU.add).then_inc(s_tab, 1)
            dve.wait_ge(s_tab, 5)
            dve.tensor_tensor(passed[:, :, :], tile_no[:, :].unsqueeze(2).to_broadcast([P, SLOT_TILES, E]),
                              tile_end[:, :].unsqueeze(1).to_broadcast([P, SLOT_TILES, E]),
                              ALU.is_ge).then_inc(s_tab, 1)
            dve.wait_ge(s_tab, 6)
            dve.tensor_tensor(jumped[:, :, :], passed[:, :, :],
                              jump[:, :].unsqueeze(1).to_broadcast([P, SLOT_TILES, E]), ALU.mult).then_inc(s_tab, 1)
            dve.wait_ge(s_tab, 7)
            dve.tensor_reduce(jumps[:, :], jumped[:, :, :], AX.X, ALU.add).then_inc(s_tab, 1)
            dve.wait_ge(s_tab, 8)
            dve.scalar_tensor_tensor(out=tile_base[:, :], in0=tile_no[:, :], scalar=float(S), in1=jumps[:, :],
                                     op0=ALU.mult, op1=ALU.add).then_inc(s_tab, 1)
            dve.wait_ge(s_tab, 9)
            dve.tensor_copy(base_int[:, :], tile_base[:, :]).then_inc(s_base, 1)
            dve.tensor_reduce(tile_expert[:, :], passed[:, :, 0:E - 1], AX.X, ALU.add).then_inc(s_tab, 1)
            dve.wait_ge(s_tab, 10)
            dve.tensor_copy(expert_int[:, :], tile_expert[:, :]).then_inc(s_expert, 1)

            dve.tensor_tensor(gate_exp[:, :, :], sorted_logits[:, :, :],
                              sorted_logits[:, :, 0:1].to_broadcast([P, TILES, E]), ALU.subtract).then_inc(s_gate, 1)
            dve.wait_ge(s_gexp, 1)
            dve.tensor_reduce(gate_sum[:, :], gate_exp[:, :, :], AX.X, ALU.add)
            dve.tensor_tensor(gate_den[:, 0, :], gate_exp[:, :, 0], gate_exp[:, :, 1], ALU.add).then_inc(s_gate, 1)
            dve.wait_ge(s_gate, 2)
            dve.scalar_tensor_tensor(out=gate_den[:, 1, :], in0=gate_sum[:, :], scalar=GATE_EPS, in1=gate_den[:, 0, :],
                                     op0=ALU.mult, op1=ALU.add).then_inc(s_gate, 1)
            dve.wait_ge(s_gate, 3)
            dve.reciprocal(gate_inv[:, :], gate_den[:, 1, :]).then_inc(s_gate, 1)
            dve.wait_ge(s_gate, 4)
            for c in range(TOP):
                ins = dve.tensor_tensor(gates[:, c, :], gate_exp[:, :, c], gate_inv[:, :], ALU.mult)
            ins.then_inc(s_gate, 1)
            dve.wait_ge(s_gate, 5)

            def weights_low(i, expert):
                r = i.ring(2)
                dve.wait_ge(s_uphi, i.plus(1).n)
                dve.tensor_tensor(up_lo[:, r, :], ew13_sb[:, bass.ds(expert * (2 * EHP), 2 * EHP)],
                                  up_hi[:, r, :].bitcast(F32), ALU.subtract).then_inc(s_uplo, 1)

            def rows_low(i):
                r = i.ring(2)
                dve.wait_ge(s_xhi, i.plus(1).n)
                dve.tensor_tensor(rows_lo[:, r, :], slots_ps, rows_hi[:, r, :].bitcast(F32),
                                  ALU.subtract).then_inc(s_xlo, 1)

            def product(i):
                r = i.ring(2)
                dve.wait_ge(s_silu1, i.plus(1).n)
                dve.wait_ge(s_h3, i.plus(1).n)
                dve.tensor_tensor(prod[:, r, :], h3_ps[r], silu1[:, r, :], ALU.mult).then_inc(s_prod, 1)

            def keep_result(i):
                dve.wait_ge(s_yy, i.plus(1).n)
                if positive(i.turn(4)):
                    dve.wait_ge(s_resout[i.ring(4)], i.turn(4) * (16 * ST))
                dve.tensor_copy(result[:, i.ring(4), :, :].rearrange("p h d -> p (h d)"),
                                result_ps).then_inc(s_res, 1)

            def expert_step(i, next_expert):
                if i.plus(-2).within(SLOT_TILES):
                    keep_result(i.plus(-2))
                if i.plus(1).within(SLOT_TILES):
                    weights_low(i.plus(1), next_expert)
                    rows_low(i.plus(1))
                if i.within(SLOT_TILES):
                    product(i)

            run_expert_steps(dve, mybir.EngineType.DVE, 1, expert_step)

            def add_choices(g):
                r = g.ring(4)
                dve.wait_ge(s_picked[r], g.turn(4) * 32 + 32)
                for c, done in ((0, s_sum1), (1, s_sum2)):
                    for t in range(FG):
                        mine = tokens[:, g.n * FG + t, :]
                        ins = dve.scalar_tensor_tensor(
                            out=mine, in0=picked[:, r, c, t, :], scalar=gates[:, c, bass.ds(g.n * FG + t, 1)],
                            in1=mine, op0=ALU.mult, op1=ALU.add)
                    ins.then_inc(done, 1)
                    dve.wait_ge(done, g.plus(1).n)

            with dve.Fori(0, TILES // FG // UNROLL) as k:
                for q in range(UNROLL):
                    add_choices(Step(k, q))


def kernel(x, adj, L0_gnn_epsilon, L0_gnn_W1, L0_gnn_b1, L0_gnn_rms_weight, L0_gnn_W2, L0_gnn_b2,
           L0_ffn_router_w, L0_ffn_w1, L0_ffn_w2, L0_ffn_w3):
    import numpy as np
    from concourse import bacc
    from concourse.bass_utils import run_bass_kernel_spmd

    def up_weights(w):
        padded = np.zeros((D, E, EHP), w.dtype)
        padded[:, :, :EH] = np.transpose(w, (2, 0, 1))
        return padded

    def down_weights(w):
        padded = np.zeros((E, EHP, D), w.dtype)
        padded[:, :EH] = np.transpose(w, (0, 2, 1))
        return np.transpose(padded.reshape(E, CHUNKS, HK, D), (2, 0, 1, 3)).reshape(HK, E * CHUNKS * D)

    a = {k: np.asarray(v) for k, v in dict(
        x=x, adj=adj, eps=L0_gnn_epsilon, w1=L0_gnn_W1, b1=L0_gnn_b1, rms_w=L0_gnn_rms_weight, w2=L0_gnn_W2,
        b2=L0_gnn_b2, router=L0_ffn_router_w, ew1=L0_ffn_w1, ew2=L0_ffn_w2, ew3=L0_ffn_w3).items()}
    arrays = dict(
        x=a["x"].reshape(TOKENS, D),
        adj_t=np.transpose(a["adj"], (0, 2, 1)).reshape(TOKENS, N),
        eps=np.broadcast_to(a["eps"].reshape(1, 1), (P, 1)),
        w1=a["w1"],
        biases=np.broadcast_to(np.concatenate([a["b1"], a["b2"]])[None], (3, H + D)),
        rms_w=np.broadcast_to(a["rms_w"][None], (P, H)),
        w2=a["w2"],
        router_t=a["router"].T,
        ew13=np.stack([up_weights(a["ew1"]), up_weights(a["ew3"])], axis=2).reshape(D, E * 2 * EHP),
        ew2=down_weights(a["ew2"]),
    )
    arrays = {f"in_{k}": np.ascontiguousarray(v) for k, v in arrays.items()}
    nc = bacc.Bacc("TRN2", target_bir_lowering=False, num_devices=1)
    ap = {k[3:]: nc.dram_tensor(k, v.shape, F32, kind="ExternalInput").ap() for k, v in arrays.items()}
    out = nc.dram_tensor("out", (TOKENS, D), F32, kind="ExternalOutput").ap()
    graph_moe_kernel(nc, ap["x"], ap["adj_t"], ap["eps"], ap["w1"], ap["biases"], ap["rms_w"], ap["w2"],
                     ap["router_t"], ap["ew13"], ap["ew2"], out)
    r = run_bass_kernel_spmd(nc, [arrays], core_ids=[0])
    return r.results[0]["out"].reshape(GRAPHS, N, D)
```

```python
from contextlib import ExitStack

import concourse.bass as bass
from concourse import mybir

F32 = mybir.dt.float32
F32R = mybir.dt.float32r
BF16 = mybir.dt.bfloat16
I32 = mybir.dt.int32
U32 = mybir.dt.uint32
ALU = mybir.AluOpType
ACT = mybir.ActivationFunctionType
AX = mybir.AxisListType

P = 128
D = 128
N = 256
GRAPHS = 32
TOKENS = GRAPHS * N
TT = N // P
TILES = TOKENS // P
H = 512
HC = H // P
BIAS = H + D
E = 8
EH = 341
EHP = EH + 1
CHUNKS = 3
HK = EHP // CHUNKS
TOP = 2
ROW = D + 2
ST = 2
S = ST * P
CAP = TOKENS + S
REGION_TILES = TOKENS // S
PADS = 2 * E - 1
SLOT_TILES = TOKENS * TOP // S + E - 1
LN_EPS, RMS_EPS, GATE_EPS = 1e-5, 1e-6, 1e-9
UNROLL = 4


class Step:

    def __init__(self, k, off):
        self.k, self.off = k, off

    @property
    def n(self):
        return self.k * UNROLL + self.off

    def ring(self, r):
        return self.off % r

    def turn(self, r):
        return self.k * (UNROLL // r) + self.off // r

    def plus(self, d):
        return Step(self.k, self.off + d)

    def within(self, count):
        return not isinstance(self.k, int) or 0 <= self.k * UNROLL + self.off < count


def positive(value):
    return not isinstance(value, int) or value > 0


def run_steps(eng, first, steady, bodies, last, step):
    for j in range(first, steady):
        step(Step(0, j))
    with eng.Fori(0, bodies) as k:
        for q in range(UNROLL):
            step(Step(k, steady + q))
    for j in range(steady + UNROLL * bodies, last + 1):
        step(Step(0, j))


def graph_moe_kernel(nc, x, adj_t, eps, w1, biases, rms_w, w2, router_t, ew13, ew2, out):
    ctx = ExitStack()
    with ctx:
        def sb(name, shape, dt=F32):
            return ctx.enter_context(nc.sbuf_tensor(name, shape, dt))

        def bank(name, shape, dt=F32):
            return ctx.enter_context(nc.psum_tensor(name, shape, dt))

        def sem(name):
            return ctx.enter_context(nc.semaphore(name))

        expert_rows = nc.dram_tensor("expert_rows", (E * CAP + (E - 1) * S, ROW), F32, kind="Internal").ap()
        results = nc.dram_tensor("results", (TOP * TOKENS + PADS * S, D), F32, kind="Internal").ap()

        bias_rows = nc.dram_tensor("bias_rows", (3, BIAS), BF16, kind="Internal").ap()

        ident = sb("ident", [P, P])
        eps_ident = sb("eps_ident", [P, P])
        eps_col = sb("eps_col", [P, 1])
        before = sb("before", [P, P], BF16)
        ones = sb("ones", [P, P], BF16)
        minus_half = sb("minus_half", [P, 3 * TT])
        expert_no = sb("expert_no", [P, E])
        region = sb("region", [P, E])
        result_no = sb("result_no", [P, TOP, TILES], I32)
        w1_sb = sb("w1_sb", [P, H])
        w1_hi = sb("w1_hi", [P, H], F32R)
        w1_lo = sb("w1_lo", [P, H], F32R)
        rms_w_sb = sb("rms_w_sb", [P, H])
        w2_sb = sb("w2_sb", [P, HC, D])
        router_sb = sb("router_sb", [P, E])
        assert BIAS % P == 0
        bias_sb = sb("bias_sb", [P, BIAS // P])
        bias_rest = sb("bias_rest", [P, 2, BIAS // P])
        bias_part = sb("bias_part", [P, 3, BIAS // P], BF16)
        bias_cut = sb("bias_cut", [3, BIAS], BF16)
        tokens = sb("tokens", [P, TILES, D])
        adj = sb("adj", [P, 2, TT, N])
        stats = sb("stats", [P, 2 * TT, 6])
        mean_var = sb("mean_var", [P, 2, 2 * TT, 2])
        spreads = sb("spreads", [P, 2, 3 * TT])
        inverse = sb("inverse", [P, 2, 3 * TT])
        shift = sb("shift", [P, 2, 2 * TT])
        normed = sb("normed", [P, 2, TT, D])
        agg_hi = sb("agg_hi", [P, 2, N], F32R)
        agg_lo = sb("agg_lo", [P, 2, N], F32R)
        squares = sb("squares", [P, TT, H])
        mean_sq = sb("mean_sq", [P, 2, TT])
        scaled = sb("scaled", [P, 2, TT, H])
        hidden_t = sb("hidden_t", [P, 2, TT, HC, P])
        rows = sb("rows", [P, 4, TOP, TT, ROW])
        normed2_t = sb("normed2_t", [P, 2, N])
        logits = sb("logits", [P, 2, TT, E])
        largest = sb("largest", [P, 2, TT, E])
        sorted_logits = sb("sorted_logits", [P, TILES, E])
        order = sb("order", [P, 2, TT, E], U32)
        chosen = sb("chosen", [P, 2, TOP, TT, E])
        mask = sb("mask", [P, 2, TT, E], BF16)
        taken = sb("taken", [P, TILES + 1, E], BF16)
        place = sb("place", [P, 2, TT, E])
        chosen_place = sb("chosen_place", [P, 2, TOP, TT, E])
        slot = sb("slot", [P, 4, TOP * TT], U32)
        silu_warm = sb("silu_warm", [P, 1])
        gate_exp = sb("gate_exp", [P, TILES, E])
        gate_sum = sb("gate_sum", [P, TILES])
        gate_den = sb("gate_den", [P, 2, TILES])
        gate_inv = sb("gate_inv", [P, TILES])
        gates = sb("gates", [P, TOP, TILES])
        counts = sb("counts", [P, E])
        count_int = sb("count_int", [P, E], I32)
        tile_whole = sb("tile_whole", [P, E, REGION_TILES])
        tile_limit = sb("tile_limit", [P, REGION_TILES])
        tile_count = sb("tile_count", [P, E])
        tile_end = sb("tile_end", [P, E])
        zeros8 = sb("zeros8", [P, E])
        jump = sb("jump", [P, E])
        tile_no = sb("tile_no", [P, SLOT_TILES])
        passed = sb("passed", [P, SLOT_TILES, E])
        jumped = sb("jumped", [P, SLOT_TILES, E])
        tile_expert = sb("tile_expert", [P, SLOT_TILES])
        jumps = sb("jumps", [P, SLOT_TILES])
        tile_base = sb("tile_base", [P, SLOT_TILES])
        expert_int = sb("expert_int", [P, SLOT_TILES], I32)
        base_int = sb("base_int", [P, SLOT_TILES], I32)
        padding = sb("padding", [P, PADS, ST, ROW])
        ew13_sb = sb("ew13_sb", [P, E * 2 * EHP])
        up_hi = sb("up_hi", [P, 2, 2 * EHP], F32R)
        up_lo = sb("up_lo", [P, 2, 2 * EHP], F32R)
        ew2_sb = sb("ew2_sb", [HK, E * CHUNKS * D])
        slot_rows = sb("slot_rows", [P, 4, ST, ROW])
        rows_hi = sb("rows_hi", [P, 2, S], F32R)
        rows_lo = sb("rows_lo", [P, 2, S], F32R)
        silu1 = scaled[0:HK, :, :, :].rearrange("p r t h -> p r (t h)")[:, :, 0:CHUNKS * S]
        prod = hidden_t[0:HK, :, :, :, :].rearrange("p r t c n -> p r (t c n)")[:, :, 0:CHUNKS * S]
        dest = sb("dest", [P, 4, ST], U32)
        zero_int = sb("zero_int", [P, ST], U32)
        result = sb("result", [P, 4, ST, D])
        FG = 4
        picked = ew13_sb[:, 0:4 * TOP * FG * D].rearrange(
            "p (r k t d) -> p r k t d", r=4, k=TOP, t=FG)

        up_ps = [bank(f"up_ps{r}", [P, 3 * 512]) for r in range(2)]
        agg_ps = up_ps[0][:, 0:512]
        hid_ps = [up_ps[0][:, (1 + t) * 512:(2 + t) * 512] for t in range(TT)]
        hidt_ps = [up_ps[1][:, t * 512:(t + 1) * 512] for t in range(TT)]
        y_ps = up_ps[1][:, 2 * 512:3 * 512]
        rank_ps = y_ps[:, TT * D:TT * D + TT * E]
        rowt_ps = bank("rowt_ps", [P, 512])
        route_ps = bank("route_ps", [P, 512])
        h1_ps = [up_ps[r][0:HK, 0:CHUNKS * S] for r in range(2)]
        h3_ps = [up_ps[r][0:HK, CHUNKS * S:2 * CHUNKS * S] for r in range(2)]
        result_ps = route_ps[:, 0:ST * D]
        slots_ps = rowt_ps[:, 0:S]

        s_w1 = sem("w1_loaded"); s_bias = sem("bias_loaded"); s_small = sem("small_loaded"); s_eps = sem("eps_loaded"); s_w2 = sem("w2_loaded")
        s_ew13 = sem("ew13_loaded"); s_ew2 = sem("ew2_loaded")
        s_x = [sem(f"x_loaded{r}") for r in range(4)]
        s_adjin = [sem(f"adj_loaded{r}") for r in range(2)]
        s_mem = sem("constants_set"); s_const = sem("constants_ready")
        s_bcut = sem("bias_steps"); s_biasrow = sem("bias_rows_moved"); s_w1cut = sem("w1_split"); s_epsid = sem("eps_ident_ready")
        s_adj = sem("adj_ready"); s_st1 = sem("stats1_done"); s_st2 = sem("stats2_done"); s_mv = sem("mean_var_done")
        s_var = sem("var_ready"); s_inverse = sem("inverse_ready"); s_shift = sem("shift_ready"); s_normed = sem("normed_ready")
        s_agg = sem("agg_done"); s_agghi = sem("agg_hi_ready"); s_agglo = sem("agg_lo_ready")
        s_hid = sem("hidden_done"); s_sq = sem("squares_done"); s_msq = sem("mean_sq_ready")
        s_scaled = sem("scaled_ready"); s_hidt = sem("hidden_transposed")
        s_silu = sem("silu_ready"); s_y = sem("y_done"); s_x2 = sem("tokens_updated")
        s_row0 = sem("first_rows_ready"); s_row1 = sem("second_rows_ready"); s_rowdest = sem("row_destinations_ready")
        s_rowt = sem("rows_transposed"); s_rowtc = sem("normed2_t_ready")
        s_logit = sem("logits_done"); s_logitc = sem("logits_copied"); s_route = sem("routing_steps"); s_mask = sem("mask_ready")
        s_rank = sem("rank_done"); s_place = sem("place_read"); s_slot = sem("slot_ready")
        s_sent = [sem(f"rows_sent{r}") for r in range(4)]
        s_cnt = sem("counts_done"); s_tab = sem("table_steps"); s_cplace = sem("chosen_place_ready")
        s_pad = sem("padding_ready"); s_padded = sem("padding_written"); s_cntint = sem("count_int_ready")
        s_gate = sem("gate_steps"); s_gexp = sem("gate_exp_ready")
        s_uphi = sem("up_hi_ready")
        s_slotrow = [sem(f"slot_rows_loaded{r}") for r in range(4)]
        s_xt = sem("slot_rows_transposed"); s_xhi = sem("rows_hi_ready"); s_xlo = sem("rows_lo_ready")
        s_h1 = sem("h1_done"); s_h3 = sem("h3_done"); s_silu1 = sem("silu1_ready"); s_dest = sem("dest_ready")
        s_prod = sem("prod_ready"); s_base = sem("bases_ready"); s_expert = sem("tile_experts_ready")
        s_yy = sem("expert_y_done"); s_res = sem("result_ready")
        s_resout = [sem(f"results_sent{r}") for r in range(4)]
        s_picked = [sem(f"picked_loaded{r}") for r in range(4)]
        s_first = sem("first_choice_weighed"); s_second = sem("second_choice_added"); s_sum = sem("sum_ready")
        s_out = [sem(f"out_written{r}") for r in range(4)]

        G = dict(first=-4, steady=8, bodies=(GRAPHS - 4 - 8) // UNROLL, last=GRAPHS + 3)
        X = dict(first=-1, steady=7, bodies=(SLOT_TILES - 1 - 7) // UNROLL, last=SLOT_TILES + 1)

        def run_expert_steps(eng, kind, ahead, step):
            def some(i, count):
                low = max(0, -ahead - i.off) if isinstance(i.k, int) else 0
                high = min(count, SLOT_TILES - ahead - i.off) if isinstance(i.k, int) else count
                experts = [None] * count
                if low < high:
                    _, experts[low:high] = nc.values_load_multi_w_load_instructions(
                        expert_int[0:1, bass.ds(i.plus(low + ahead).n, high - low)], engines=[kind], min_val=0,
                        max_val=E - 1, skip_runtime_bounds_check_because="sums of E - 1 comparisons")
                for q in range(count):
                    step(i.plus(q), experts[q])

            for j in range(X["first"], X["steady"], UNROLL):
                some(Step(0, j), UNROLL)
            with eng.Fori(0, X["bodies"]) as k:
                some(Step(k, X["steady"]), UNROLL)
            for j in range(X["steady"] + UNROLL * X["bodies"], X["last"] + 1, UNROLL):
                some(Step(0, j), min(UNROLL, X["last"] + 1 - j))

        def has_inverse(j):
            return j.plus(3).within(GRAPHS) or j.plus(-2).within(GRAPHS)

        def inverse_columns(j):
            first = 0 if j.plus(3).within(GRAPHS) else TT
            last = 3 * TT if j.within(GRAPHS) else 2 * TT if j.plus(-2).within(GRAPHS) else TT
            return slice(first, last)

        block = ctx.enter_context(nc.Block())

        @block.sync
        def _(sp):
            def load_x(u):
                sp.dma_start(tokens[:, bass.ds(u.n * TT, TT), :],
                             x.rearrange("(t p) d -> p t d", p=P)[:, bass.ds(u.n * TT, TT), :]
                             ).then_inc(s_x[u.ring(4)], 16)

            def load_adj(u):
                if positive(u.plus(-1).n):
                    sp.wait_ge(s_agg, u.plus(-1).n)
                sp.dma_start(adj[:, u.ring(2), :, :],
                             adj_t.rearrange("(b c p) n -> p b c n", p=P, c=TT)[:, bass.ds(u.n, 1), :, :]
                             .rearrange("p b c n -> p (b c) n")
                             ).then_inc(s_adjin[u.ring(2)], 16)

            def load_step(u):
                load_adj(u)
                if u.plus(2).within(GRAPHS):
                    load_x(u.plus(2))

            load_x(Step(0, 0))
            load_x(Step(0, 1))
            load_step(Step(0, 0))
            load_step(Step(0, 1))
            sp.wait_ge(s_bcut, 5)
            sp.dma_start(bias_rows.rearrange("i (p f) -> p i f", p=P), bias_part[:, :, :]).then_inc(s_biasrow, 16)
            sp.wait_ge(s_biasrow, 16)
            sp.dma_start(bias_cut[:, :], bias_rows).then_inc(s_biasrow, 16)
            sp.dma_start(w2_sb[:, :, :], w2.rearrange("(c p) d -> p c d", p=P)).then_inc(s_w2, 16)
            load_step(Step(0, 2))
            load_step(Step(0, 3))
            PIECES = GRAPHS // UNROLL - 2
            with sp.Fori(1, 1 + PIECES) as k:
                for q in range(UNROLL):
                    load_step(Step(k, q))
                for weights, kept, loaded in ((ew13, ew13_sb, s_ew13), (ew2, ew2_sb, s_ew2)):
                    piece = kept.shape[1] // PIECES
                    at = bass.ds(k * piece - piece, piece)
                    sp.dma_start(kept[:, at], weights[:, at]).then_inc(loaded, 16)
            for u in range(GRAPHS - UNROLL, GRAPHS):
                load_step(Step(0, u))

            sp.wait_ge(s_pad, 1)
            sp.dma_start(expert_rows[E * CAP:E * CAP + (E - 1) * S, :].rearrange("(b p h) r -> p b h r", p=P, h=ST),
                         padding[:, E:PADS, :, :]).then_inc(s_padded, 16)
            sp.wait_ge(s_cntint, 1)
            _, found = nc.values_load_multi_w_load_instructions(
                count_int[0:1, :], engines=[mybir.EngineType.SP], min_val=0, max_val=TOKENS,
                skip_runtime_bounds_check_because="an expert has at most one row of every token")
            for e in range(E):
                sp.dma_start(expert_rows[bass.ds(found[e] + e * CAP, S), :].rearrange("(p h) r -> p h r", h=ST),
                             padding[:, e, :, :]).then_inc(s_padded, 16)

            def bases_of(i, count):
                _, bases = nc.values_load_multi_w_load_instructions(
                    base_int[0:1, bass.ds(i.n, count)], engines=[mybir.EngineType.SP], min_val=0,
                    max_val=E * CAP + (E - 2) * S,
                    skip_runtime_bounds_check_because="the list holds SLOT_TILES tiles, each within its region")
                return bases

            def load_slots(i, base):
                if positive(i.plus(-3).n):
                    sp.wait_ge(s_xt, i.plus(-3).n)
                    sp.wait_ge(s_dest, i.plus(-3).n)
                sp.dma_start(slot_rows[:, i.ring(4), :, :],
                             expert_rows[bass.ds(base, S), :].rearrange("(p h) r -> p h r", h=ST)
                             ).then_inc(s_slotrow[i.ring(4)], 16)

            def load_some(i, bases):
                for q, base in enumerate(bases):
                    load_slots(i.plus(q), base)

            sp.wait_ge(s_base, 1)
            first_bases = bases_of(Step(0, 0), UNROLL)
            sp.wait_ge(s_padded, 16 * (E + 1))
            for r in range(4):
                sp.wait_ge(s_sent[r], 16 * TOP * TT * (GRAPHS // 4))
            load_some(Step(0, 0), first_bases)
            with sp.Fori(1, SLOT_TILES // UNROLL) as k:
                load_some(Step(k, 0), bases_of(Step(k, 0), UNROLL))
            left = SLOT_TILES % UNROLL
            load_some(Step(0, SLOT_TILES - left), bases_of(Step(0, SLOT_TILES - left), left))

            for r in range(4):
                sp.wait_ge(s_resout[r], 16 * ST * ((SLOT_TILES + 3 - r) // 4))
            STEPS = TILES // FG
            picks = results[0:TOP * TOKENS, :].rearrange("(k t p) d -> p k t d", p=P, k=TOP)
            out_t = out.rearrange("(t p) d -> p t d", p=P)

            def load_picked(g):
                for c in range(TOP):
                    sp.dma_start(picked[:, g.ring(4), c, :, :],
                                 picks[:, c, bass.ds(g.n * FG, FG), :]).then_inc(s_picked[g.ring(4)], 16)

            def store(g):
                sp.wait_ge(s_sum, g.plus(1).n)
                sp.dma_start(out_t[:, bass.ds(g.n * FG, FG), :],
                             tokens[:, bass.ds(g.n * FG, FG), :]).then_inc(s_out[g.ring(4)], 16)

            for q in range(UNROLL):
                load_picked(Step(0, q))
            with sp.Fori(0, STEPS // UNROLL - 1) as k:
                for q in range(UNROLL):
                    store(Step(k, q))
                    load_picked(Step(k, q + 4))
            for q in range(STEPS - UNROLL, STEPS):
                store(Step(0, q))
            for r in range(4):
                sp.wait_ge(s_out[r], 16 * (STEPS // 4))

        @block.gpsimd
        def _(pool):
            pool.memset(ident[:, :], 0.0).then_inc(s_mem, 1)
            pool.memset(before[:, :], 1.0).then_inc(s_mem, 1)
            pool.memset(ones[:, :], 1.0).then_inc(s_const, 1)
            pool.memset(minus_half[:, :], -0.5).then_inc(s_const, 1)
            pool.wait_ge(s_mem, 2)
            pool.affine_select(out=ident[:, :], in_=ident[:, :], compare_op=ALU.not_equal, fill=1.0,
                               base=0, pattern=[[-1, P]], channel_multiplier=1).then_inc(s_const, 1)
            pool.affine_select(out=before[:, :], in_=before[:, :], compare_op=ALU.is_gt, fill=0.0,
                               base=0, pattern=[[1, P]], channel_multiplier=-1).then_inc(s_const, 1)
            pool.iota(expert_no[:, :], pattern=[[1, E]], base=0, channel_multiplier=0,
                      allow_small_or_imprecise_dtypes=True).then_inc(s_const, 1)
            pool.iota(result_no[:, :, :], pattern=[[TOKENS, TOP], [P, TILES]], base=0, channel_multiplier=1).then_inc(s_const, 1)
            pool.iota(region[:, :], pattern=[[CAP, E]], base=0, channel_multiplier=0,
                      allow_small_or_imprecise_dtypes=True).then_inc(s_const, 1)
            pool.iota(tile_no[:, :], pattern=[[1, SLOT_TILES]], base=0, channel_multiplier=0,
                      allow_small_or_imprecise_dtypes=True).then_inc(s_const, 1)
            pool.iota(tile_limit[:, :], pattern=[[S, REGION_TILES]], base=0, channel_multiplier=0,
                      allow_small_or_imprecise_dtypes=True).then_inc(s_const, 1)
            pool.memset(taken[:, 0, :], 0.0).then_inc(s_const, 1)
            pool.memset(zeros8[:, :], 0.0)
            pool.memset(zero_int[:, :], 0).then_inc(s_const, 1)
            pool.memset(rows[:, :, :, :, D + 1:ROW], 0.0).then_inc(s_const, 1)
            pool.memset(mean_var[:, :, :, :], 1.0)
            pool.memset(spreads[:, :, :], 1.0).then_inc(s_const, 1)

            def inverse_of(j):
                r = j.ring(2)
                pool.wait_ge(s_var, j.plus(4).n)
                if j.within(GRAPHS):
                    pool.wait_ge(s_msq, j.plus(1).n)
                at = inverse_columns(j)
                pool.tensor_tensor(inverse[:, r, at], spreads[:, r, at], minus_half[:, at], ALU.pow).then_inc(s_inverse, 1)

            def add_epsilon(u):
                pool.wait_ge(s_adjin[u.ring(2)], u.turn(2) * 16 + 16)
                blocks = adj[:, u.ring(2), :, :].rearrange("p c (b n) -> p (c b) n", n=P)[:, 0:TT * TT:TT + 1, :]
                pool.tensor_tensor(blocks, blocks, eps_ident[:, :].unsqueeze(1).to_broadcast([P, TT, P]),
                                   ALU.add).then_inc(s_adj, 1)

            def send(u):
                r = u.ring(4)
                for n in range(TOP * TT):
                    pool.indirect_dma_start(
                        out=expert_rows, out_offset=bass.IndirectOffsetOnAxis(ap=slot[:, r, n:n + 1], axis=0),
                        in_=rows[:, r, n // TT, n % TT, :], in_offset=None).then_inc(s_sent[r], 16)

            def step(j):
                if has_inverse(j):
                    inverse_of(j)
                sent = j.plus(-4)
                if sent.within(GRAPHS):
                    pool.wait_ge(s_slot, sent.plus(1).n)
                    pool.wait_ge(s_row1, sent.plus(1).n)
                    pool.wait_ge(s_rowdest, sent.plus(1).n)
                if j.plus(3).within(GRAPHS):
                    if isinstance(j.k, int) and j.off == -3:
                        pool.wait_ge(s_epsid, 1)
                    add_epsilon(j.plus(3))
                if sent.within(GRAPHS):
                    send(sent)
                piece = j.off - G["first"] if isinstance(j.k, int) else E
                if piece < E:
                    at = slice(piece * ST, min((piece + 1) * ST, PADS))
                    pool.memset(padding[:, at, :, :], 0.0).then_inc(s_mem, 1)
                if piece == E - 1:
                    pool.wait_ge(s_mem, 2 + E)
                    pool.iota(padding[:, :, :, D].bitcast(I32), pattern=[[S, PADS], [P, ST]], base=TOP * TOKENS,
                              channel_multiplier=1).then_inc(s_pad, 1)

            pool.wait_ge(s_const, 13)
            run_steps(pool, G["first"], G["steady"], G["bodies"], G["last"], step)

            def destinations(i):
                q = i.ring(4)
                pool.wait_ge(s_slotrow[q], i.turn(4) * 16 + 16)
                if positive(i.turn(4)):
                    pool.wait_ge(s_resout[q], i.turn(4) * (16 * ST))
                pool.tensor_tensor(dest[:, q, :], slot_rows[:, q, :, D].bitcast(U32), zero_int[:, :],
                                   ALU.add).then_inc(s_dest, 1)

            def send_result(i, ahead):
                pool.wait_ge(s_res, i.plus(1).n)
                pool.wait_ge(s_dest, i.plus(1).n)
                if ahead.within(SLOT_TILES):
                    destinations(ahead)
                r = i.ring(4)
                for h in range(ST):
                    pool.indirect_dma_start(
                        out=results, out_offset=bass.IndirectOffsetOnAxis(ap=dest[:, r, h:h + 1], axis=0),
                        in_=result[:, r, h, :], in_offset=None).then_inc(s_resout[r], 16)

            def expert_step(i):
                if i.within(SLOT_TILES):
                    send_result(i, i.plus(2))
                else:
                    destinations(i.plus(2))

            run_steps(pool, -2, 4, (SLOT_TILES - 2 - 4) // UNROLL, SLOT_TILES - 1, expert_step)

        @block.scalar
        def _(act):
            act.dma_start(eps_col[:, :], eps).then_inc(s_eps, 16)
            act.dma_start(bias_sb[:, :], biases).then_inc(s_bias, 16)
            act.dma_start(w1_sb[:, :], w1).then_inc(s_w1, 16)
            act.wait_ge(s_const, 1)
            act.activation(silu_warm[:, :], ones[:, 0:1], ACT.Silu)
            act.dma_start(rms_w_sb[:, :], rms_w).then_inc(s_small, 16)
            act.dma_start(router_sb[:, :], router_t).then_inc(s_small, 16)

            def agg_high(u):
                act.wait_ge(s_agg, u.plus(1).n)
                act.activation(agg_hi[:, u.ring(2), :], agg_ps[:, 0:N], ACT.Copy).then_inc(s_agghi, 1)

            def silu_of(u):
                r = u.ring(2)
                for t in range(TT):
                    act.wait_ge(s_hidt, u.n * TT + t + 1)
                    act.activation(hidden_t[:, r, t, :, :].rearrange("p c n -> p (c n)"), hidt_ps[t][:, :],
                                   ACT.Silu).then_inc(s_silu, 1)

            def normalise(out_of, u, at, j):
                r = j.ring(2)
                for t in range(TT):
                    ins = act.activation(out_of(t), tokens[:, u.n * TT + t, :], ACT.Identity,
                                         bias=shift[:, r, at + t:at + t + 1], scale=inverse[:, r, at + t:at + t + 1])
                return ins

            def square_of(u, t):
                act.wait_ge(s_hid, u.n * TT + t + 1)
                if positive(u.n):
                    act.wait_ge(s_sq, u.n * TT + t - 1)
                act.activation(squares[:, t, :], hid_ps[t][:, :], ACT.Square, scale=float(H) ** -0.5,
                               accum_out=mean_sq[:, u.ring(2), t:t + 1]).then_inc(s_sq, 1)

            def rows_t(u):
                act.wait_ge(s_rowt, u.plus(1).n)
                act.activation(normed2_t[:, u.ring(2), :], rowt_ps[:, 0:N], ACT.Copy).then_inc(s_rowtc, 1)

            def step(j):
                if j.plus(2).within(GRAPHS):
                    agg_high(j.plus(2))
                if has_inverse(j):
                    act.wait_ge(s_shift, j.plus(4).n)
                ended = j.plus(-2)
                q = ended.ring(4)
                if ended.within(GRAPHS):
                    if positive(ended.turn(4)):
                        act.wait_ge(s_sent[q], ended.turn(4) * (16 * TOP * TT))
                    normalise(lambda t: rows[:, q, 0, t, 0:D], ended, TT, j).then_inc(s_row0, 1)
                if j.plus(3).within(GRAPHS):
                    normalise(lambda t: normed[:, j.plus(3).ring(2), t, :], j.plus(3), 0, j).then_inc(s_normed, 1)
                if ended.within(GRAPHS):
                    act.wait_ge(s_row0, ended.plus(1).n)
                    act.activation(rows[:, q, 1, :, 0:D], rows[:, q, 0, :, 0:D], ACT.Copy).then_inc(s_row1, 1)
                if j.plus(1).within(GRAPHS):
                    for t in range(TT):
                        square_of(j.plus(1), t)
                if ended.within(GRAPHS):
                    rows_t(ended)
                if j.within(GRAPHS):
                    silu_of(j)

            act.wait_ge(s_w1, 16)
            act.activation(w1_hi[:, :], w1_sb[:, :], ACT.Copy).then_inc(s_w1cut, 1)
            act.wait_ge(s_const, 13)
            run_steps(act, G["first"], G["steady"], G["bodies"], G["last"], step)

            act.wait_ge(s_gate, 1)
            act.activation(gate_exp[:, :, :], gate_exp[:, :, :], ACT.Exp).then_inc(s_gexp, 1)
            act.activation(silu_warm[:, :], shift[:, 0, 0:1], ACT.Silu)

            act.wait_ge(s_ew13, 16 * (GRAPHS // UNROLL - 2))
            act.wait_ge(s_expert, 1)

            def weights_high(i, expert):
                if positive(i.plus(-1).n):
                    act.wait_ge(s_h3, i.plus(-1).n)
                act.activation(up_hi[:, i.ring(2), :], ew13_sb[:, bass.ds(expert * (2 * EHP), 2 * EHP)],
                               ACT.Copy).then_inc(s_uphi, 1)

            def silu_h1(i):
                r = i.ring(2)
                act.wait_ge(s_h1, i.plus(1).n)
                act.activation(silu1[:, r, :], h1_ps[r], ACT.Silu).then_inc(s_silu1, 1)

            def rows_high(i):
                act.wait_ge(s_xt, i.plus(1).n)
                act.activation(rows_hi[:, i.ring(2), :], slots_ps, ACT.Copy).then_inc(s_xhi, 1)

            def expert_step(i, next_expert):
                if i.plus(1).within(SLOT_TILES):
                    weights_high(i.plus(1), next_expert)
                if i.within(SLOT_TILES):
                    silu_h1(i)
                if i.plus(1).within(SLOT_TILES):
                    rows_high(i.plus(1))

            run_expert_steps(act, mybir.EngineType.Activation, 1, expert_step)

            act.wait_ge(s_gate, 5)

            def weigh_first(g):
                r = g.ring(4)
                act.wait_ge(s_picked[r], g.turn(4) * 32 + 32)
                for t in range(FG):
                    ins = act.activation(picked[:, r, 0, t, :], picked[:, r, 0, t, :], ACT.Copy,
                                         scale=gates[:, 0, bass.ds(g.n * FG + t, 1)])
                ins.then_inc(s_first, 1)

            with act.Fori(0, TILES // FG // UNROLL) as k:
                for q in range(UNROLL):
                    weigh_first(Step(k, q))

        @block.tensor
        def _(pe):
            def sum_neighbours(u):
                r = u.ring(2)
                pe.wait_ge(s_normed, u.plus(1).n)
                pe.wait_ge(s_adj, u.plus(1).n)
                if positive(u.n):
                    pe.wait_ge(s_agglo, u.n)
                for c in range(TT):
                    ins = pe.matmul(agg_ps[:, 0:N], normed[:, r, c, :], adj[:, r, c, :], start=(c == 0), stop=(c == TT - 1))
                ins.then_inc(s_agg, 1)

            def transpose_hidden(u):
                for t in range(TT):
                    pe.wait_ge(s_scaled, u.n * TT + t + 1)
                    for c in range(HC):
                        ins = pe.transpose(hidt_ps[t][:, c * P:(c + 1) * P],
                                           scaled[:, u.ring(2), t, c * P:(c + 1) * P], ident[:, :])
                    ins.then_inc(s_hidt, 1)

            def first_product(u):
                r = u.ring(2)
                pe.wait_ge(s_agglo, u.plus(1).n)
                for t in range(TT):
                    if positive(u.n):
                        pe.wait_ge(s_scaled, u.n * TT + t - 1)
                    hi, lo = agg_hi[:, r, t * P:(t + 1) * P], agg_lo[:, r, t * P:(t + 1) * P]
                    pe.matmul(hid_ps[t][:, :], ones[0:3, :], bias_cut[:, 0:H], start=True, stop=False)
                    pe.matmul(hid_ps[t][:, :], lo, w1_hi[:, :], start=False, stop=False)
                    pe.matmul(hid_ps[t][:, :], hi, w1_lo[:, :], start=False, stop=False)
                    pe.matmul(hid_ps[t][:, :], hi, w1_hi[:, :], start=False, stop=True).then_inc(s_hid, 1)

            def second_product(u):
                pe.wait_ge(s_silu, u.n * TT + TT)
                if positive(u.n):
                    pe.wait_ge(s_x2, u.n)
                if positive(u.plus(-2).n):
                    pe.wait_ge(s_place, u.plus(-2).n)
                for t in range(TT):
                    pe.matmul(y_ps[:, t * D:(t + 1) * D], ones[0:3, :], bias_cut[:, H:H + D], start=True, stop=False)
                    for c in range(HC):
                        ins = pe.matmul(y_ps[:, t * D:(t + 1) * D], hidden_t[:, u.ring(2), t, c, :], w2_sb[:, c, :],
                                        start=False, stop=(c == HC - 1))
                ins.then_inc(s_y, 1)

            def transpose_rows(u):
                pe.wait_ge(s_row0, u.plus(1).n)
                for t in range(TT):
                    ins = pe.transpose(rowt_ps[:, t * P:(t + 1) * P], rows[:, u.ring(4), 0, t, 0:D], ident[:, :])
                ins.then_inc(s_rowt, 1)

            def router(u):
                pe.wait_ge(s_rowtc, u.plus(1).n)
                if positive(u.n):
                    pe.wait_ge(s_logitc, u.n)
                for t in range(TT):
                    ins = pe.matmul(route_ps[:, t * E:(t + 1) * E], normed2_t[:, u.ring(2), t * P:(t + 1) * P],
                                    router_sb[:, :], start=True, stop=True)
                ins.then_inc(s_logit, 1)

            def rank(u):
                pe.wait_ge(s_mask, u.plus(1).n)
                for t in range(TT):
                    part = rank_ps[:, t * E:(t + 1) * E]
                    pe.matmul(part, before[:, :], mask[:, u.ring(2), t, :], start=True, stop=False)
                    ins = pe.matmul(part, ones[:, :], taken[:, u.n * TT + t, :], start=False, stop=True)
                ins.then_inc(s_rank, 1)

            def step(j):
                if j.plus(2).within(GRAPHS):
                    sum_neighbours(j.plus(2))
                if j.plus(-1).within(GRAPHS):
                    second_product(j.plus(-1))
                if j.plus(1).within(GRAPHS):
                    first_product(j.plus(1))
                if j.plus(-2).within(GRAPHS):
                    transpose_rows(j.plus(-2))
                if j.within(GRAPHS):
                    transpose_hidden(j)
                if j.plus(-3).within(GRAPHS):
                    rank(j.plus(-3))
                if j.plus(-2).within(GRAPHS):
                    router(j.plus(-2))

            def keep_busy(count):
                for _ in range(count):
                    pe.matmul(rowt_ps[:, 0:P], ident[:, :], ident[:, :], start=True, stop=True)

            pe.wait_ge(s_const, 13)
            keep_busy(12)
            step(Step(0, -2))
            pe.wait_ge(s_w1cut, 2)
            pe.wait_ge(s_biasrow, 32)
            step(Step(0, -1))
            step(Step(0, 0))
            pe.wait_ge(s_small, 32)
            pe.wait_ge(s_w2, 16)
            run_steps(pe, 1, G["steady"], G["bodies"], G["last"], step)

            pe.matmul(rowt_ps[:, 0:E], ones[:, :], taken[:, TILES, :], start=True, stop=True).then_inc(s_cnt, 1)

            pe.wait_ge(s_ew2, 16 * (GRAPHS // UNROLL - 2))
            pe.wait_ge(s_place, GRAPHS)
            pe.wait_ge(s_tab, 1)
            pe.wait_ge(s_expert, 1)
            keep_busy(13)

            def transpose_slots(i):
                pe.wait_ge(s_slotrow[i.ring(4)], i.turn(4) * 16 + 16)
                for h in range(ST):
                    ins = pe.transpose(slots_ps[:, h * P:(h + 1) * P], slot_rows[:, i.ring(4), h, 0:D],
                                       ident[:, :])
                ins.then_inc(s_xt, 1)

            def up(i):
                r = i.ring(2)
                pe.wait_ge(s_xlo, i.plus(1).n)
                for k, ps in ((0, h1_ps[r]), (1, h3_ps[r])):
                    for c in range(CHUNKS):
                        part = ps[:, c * S:(c + 1) * S]
                        at = slice(k * EHP + c * HK, k * EHP + (c + 1) * HK)
                        pe.matmul(part, up_hi[:, r, at], rows_lo[:, r, :], start=True, stop=False)
                        pe.matmul(part, up_lo[:, r, at], rows_hi[:, r, :], start=False, stop=False)
                        ins = pe.matmul(part, up_hi[:, r, at], rows_hi[:, r, :], start=False, stop=True)
                        if k == 1 and c == 0:
                            ins.then_inc(s_h1, 1)
                ins.then_inc(s_h3, 1)

            def down(i, expert):
                r = i.ring(2)
                pe.wait_ge(s_prod, i.plus(1).n)
                if positive(i.n):
                    pe.wait_ge(s_res, i.n)
                for h in range(ST):
                    for c in range(CHUNKS):
                        ins = pe.matmul(result_ps[:, h * D:(h + 1) * D],
                                        prod[:, r, c * S + h * P:c * S + (h + 1) * P],
                                        ew2_sb[:, bass.ds((expert * CHUNKS + c) * D, D)],
                                        start=(c == 0), stop=(c == CHUNKS - 1))
                ins.then_inc(s_yy, 1)

            def expert_step(i, expert_before):
                if i.within(SLOT_TILES):
                    up(i)
                if i.plus(1).within(SLOT_TILES):
                    transpose_slots(i.plus(1))
                if i.plus(-1).within(SLOT_TILES):
                    down(i.plus(-1), expert_before)

            run_expert_steps(pe, mybir.EngineType.PE, -1, expert_step)

        @block.vector
        def _(dve):
            def agg_low(u):
                r = u.ring(2)
                dve.wait_ge(s_agghi, u.plus(1).n)
                dve.tensor_tensor(agg_lo[:, r, :], agg_ps[:, 0:N], agg_hi[:, r, :].bitcast(F32),
                                  ALU.subtract).then_inc(s_agglo, 1)

            def mean_square(u):
                r = u.ring(2)
                dve.wait_ge(s_sq, u.n * TT + TT)
                dve.tensor_scalar(spreads[:, r, 2 * TT:], mean_sq[:, r, :], RMS_EPS, None, ALU.add).then_inc(s_msq, 1)

            def scale_hidden(u):
                r = u.ring(2)
                for t in range(TT):
                    dve.scalar_tensor_tensor(out=scaled[:, r, t, :], in0=hid_ps[t][:, :], scalar=inverse[:, r, 2 * TT + t:2 * TT + t + 1],
                                             in1=rms_w_sb[:, :], op0=ALU.mult, op1=ALU.mult).then_inc(s_scaled, 1)

            def step(j):
                fresh, ended, routed, placed = j.plus(4), j.plus(-1), j.plus(-3), j.plus(-4)
                is_fresh, is_ended, is_routed, is_placed = (u.within(GRAPHS) for u in (fresh, ended, routed, placed))
                has_statistics = is_fresh or is_ended
                s, r, p, q = j.ring(2), routed.ring(2), placed.ring(2), placed.ring(4)
                if j.within(GRAPHS):
                    mean_square(j)
                if is_placed:
                    dve.wait_ge(s_rank, placed.plus(1).n)
                    dve.tensor_tensor(place[:, p, :, :],
                                      rank_ps[:, 0:TT * E].rearrange("p (t e) -> p t e", t=TT),
                                      region[:, :].unsqueeze(1).to_broadcast([P, TT, E]), ALU.add).then_inc(s_place, 1)
                if is_routed:
                    dve.wait_ge(s_logit, routed.plus(1).n)
                    dve.tensor_copy(logits[:, r, :, :].rearrange("p t e -> p (t e)"),
                                    route_ps[:, 0:TT * E]).then_inc(s_logitc, 1)
                if is_routed:
                    dve.wait_ge(s_logitc, routed.plus(1).n)
                if is_placed:
                    if not is_routed:
                        dve.wait_ge(s_place, placed.plus(1).n)
                    dve.tensor_tensor(chosen_place[:, p, :, :, :], chosen[:, p, :, :, :],
                                      place[:, p, :, :].unsqueeze(1).to_broadcast([P, TOP, TT, E]),
                                      ALU.mult).then_inc(s_cplace, 1)
                if is_routed:
                    for t in range(TT):
                        ins = dve.max(largest[:, r, t, :], logits[:, r, t, :])
                    ins.then_inc(s_route, 1)
                if is_placed:
                    dve.wait_ge(s_cplace, placed.plus(1).n)
                    if positive(placed.turn(4)):
                        dve.wait_ge(s_sent[q], placed.turn(4) * (16 * TOP * TT))
                    with nc.allow_low_precision(reason="whole numbers below 2**24, added in float32: exact"):
                        dve.tensor_reduce(slot[:, q, :].rearrange("p (c t) -> p c t", c=TOP),
                                          chosen_place[:, p, :, :, :], AX.X, ALU.add).then_inc(s_slot, 1)
                if is_routed:
                    dve.wait_ge(s_route, routed.n * 5 + 1)
                    dve.tensor_copy(sorted_logits[:, bass.ds(routed.n * TT, TT), :], largest[:, r, :, :])
                    for t in range(TT):
                        ins = dve.max_index(order[:, r, t, :], largest[:, r, t, :], logits[:, r, t, :])
                    ins.then_inc(s_route, 1)
                    dve.wait_ge(s_route, routed.n * 5 + 2)
                    dve.tensor_tensor(chosen[:, r, :, :, :],
                                      expert_no[:, :].unsqueeze(1).unsqueeze(1).to_broadcast([P, TOP, TT, E]),
                                      order[:, r, :, 0:TOP].rearrange("p t c -> p c t").unsqueeze(3)
                                      .to_broadcast([P, TOP, TT, E]), ALU.is_equal).then_inc(s_route, 1)
                if has_inverse(j):
                    dve.wait_ge(s_inverse, j.plus(4).n)
                    at = slice(inverse_columns(j).start, min(2 * TT, inverse_columns(j).stop))
                    dve.scalar_tensor_tensor(out=shift[:, s, at], in0=mean_var[:, 1 - s, at, 0], scalar=-1.0,
                                             in1=inverse[:, s, at], op0=ALU.mult, op1=ALU.mult).then_inc(s_shift, 1)
                if j.within(GRAPHS):
                    scale_hidden(j)
                if is_fresh:
                    dve.wait_ge(s_x[fresh.ring(4)], fresh.turn(4) * 16 + 16)
                if j.plus(2).within(GRAPHS):
                    agg_low(j.plus(2))
                if is_fresh:
                    for t in range(TT):
                        ins = dve.bn_stats(stats[:, t, :], tokens[:, fresh.n * TT + t, :])
                    ins.then_inc(s_st1, 1)
                if is_routed:
                    dve.wait_ge(s_route, routed.n * 5 + 3)
                    dve.tensor_tensor(mask[:, r, :, :], chosen[:, r, 0, :, :], chosen[:, r, 1, :, :],
                                      ALU.add).then_inc(s_route, 1)
                if is_ended:
                    dve.wait_ge(s_y, ended.plus(1).n)
                    mine = tokens[:, bass.ds(ended.n * TT, TT), :]
                    dve.tensor_tensor(mine, y_ps[:, 0:TT * D].rearrange("p (t d) -> p t d", t=TT), mine,
                                      ALU.add).then_inc(s_x2, 1)
                if is_routed:
                    dve.wait_ge(s_route, routed.n * 5 + 4)
                    dve.tensor_tensor(taken[:, routed.n * TT + 1, :], taken[:, routed.n * TT, :], mask[:, r, 0, :],
                                      ALU.add).then_inc(s_route, 1)
                if is_ended:
                    dve.wait_ge(s_x2, ended.plus(1).n)
                if j.plus(-2).within(GRAPHS):
                    u = j.plus(-2)
                    dve.wait_ge(s_row0, u.plus(1).n)
                    dve.tensor_scalar(rows[:, u.ring(4), :, :, D].bitcast(I32), result_no[:, :, bass.ds(u.n * TT, TT)],
                                      0.0, None, ALU.add).then_inc(s_rowdest, 1)
                if is_ended:
                    for t in range(TT):
                        ins = dve.bn_stats(stats[:, TT + t, :], tokens[:, ended.n * TT + t, :])
                    ins.then_inc(s_st2, 1)
                if is_ended:
                    dve.wait_ge(s_st2, ended.plus(1).n)
                elif is_fresh:
                    dve.wait_ge(s_st1, fresh.plus(1).n)
                if is_routed:
                    if not is_ended:
                        dve.wait_ge(s_route, routed.n * 5 + 5)
                    dve.tensor_tensor(taken[:, routed.n * TT + 2, :], taken[:, routed.n * TT + 1, :], mask[:, r, 1, :],
                                      ALU.add).then_inc(s_mask, 1)
                if has_statistics:
                    for t in (range(TT) if is_fresh else ()):
                        ins = dve.bn_aggr(mean_var[:, s, t, :], stats[:, t, :])
                    for t in (range(TT, 2 * TT) if is_ended else ()):
                        ins = dve.bn_aggr(mean_var[:, s, t, :], stats[:, t, :])
                    ins.then_inc(s_mv, 1)
                    dve.wait_ge(s_mv, j.plus(5).n)
                    dve.tensor_scalar(spreads[:, 1 - s, 0:2 * TT], mean_var[:, s, :, 1], LN_EPS, None, ALU.add).then_inc(s_var, 1)

            dve.wait_ge(s_const, 13)
            step(Step(0, -4))
            dve.wait_ge(s_eps, 16)
            dve.tensor_scalar(eps_ident[:, :], ident[:, :], eps_col[:, 0:1], None, ALU.mult).then_inc(s_epsid, 1)
            dve.wait_ge(s_bias, 16)
            dve.tensor_copy(bias_part[:, 0, :], bias_sb[:, :]).then_inc(s_bcut, 1)
            dve.wait_ge(s_bcut, 1)
            dve.tensor_tensor(bias_rest[:, 0, :], bias_sb[:, :], bias_part[:, 0, :], ALU.subtract).then_inc(s_bcut, 1)
            dve.wait_ge(s_bcut, 2)
            dve.tensor_copy(bias_part[:, 1, :], bias_rest[:, 0, :]).then_inc(s_bcut, 1)
            dve.wait_ge(s_bcut, 3)
            dve.tensor_tensor(bias_rest[:, 1, :], bias_rest[:, 0, :], bias_part[:, 1, :], ALU.subtract).then_inc(s_bcut, 1)
            dve.wait_ge(s_bcut, 4)
            dve.tensor_copy(bias_part[:, 2, :], bias_rest[:, 1, :]).then_inc(s_bcut, 1)
            step(Step(0, -3))
            dve.wait_ge(s_w1cut, 1)
            dve.tensor_tensor(w1_lo[:, :], w1_sb[:, :], w1_hi[:, :].bitcast(F32), ALU.subtract).then_inc(s_w1cut, 1)
            dve.wait_ge(s_small, 32)
            run_steps(dve, -2, G["steady"], G["bodies"], G["last"], step)

            dve.wait_ge(s_cnt, 1)
            dve.tensor_copy(counts[:, :], rowt_ps[:, 0:E]).then_inc(s_tab, 1)
            dve.wait_ge(s_tab, 1)
            dve.tensor_copy(count_int[:, :], counts[:, :]).then_inc(s_cntint, 1)
            dve.tensor_tensor(tile_whole[:, :, :], counts[:, :].unsqueeze(2).to_broadcast([P, E, REGION_TILES]),
                              tile_limit[:, :].unsqueeze(1).to_broadcast([P, E, REGION_TILES]),
                              ALU.is_gt).then_inc(s_tab, 1)
            dve.wait_ge(s_tab, 2)
            dve.tensor_reduce(tile_count[:, :], tile_whole[:, :, :], AX.X, ALU.add).then_inc(s_tab, 1)
            dve.wait_ge(s_tab, 3)
            dve.tensor_tensor_scan(tile_end[:, :], tile_count[:, :], zeros8[:, :], 0.0, ALU.add,
                                   ALU.add).then_inc(s_tab, 1)
            dve.tensor_scalar(jump[:, :], tile_count[:, :], float(-S), float(CAP), ALU.mult, ALU.add).then_inc(s_tab, 1)
            dve.wait_ge(s_tab, 5)
            dve.tensor_tensor(passed[:, :, :], tile_no[:, :].unsqueeze(2).to_broadcast([P, SLOT_TILES, E]),
                              tile_end[:, :].unsqueeze(1).to_broadcast([P, SLOT_TILES, E]),
                              ALU.is_ge).then_inc(s_tab, 1)
            dve.wait_ge(s_tab, 6)
            dve.tensor_tensor(jumped[:, :, :], passed[:, :, :],
                              jump[:, :].unsqueeze(1).to_broadcast([P, SLOT_TILES, E]), ALU.mult).then_inc(s_tab, 1)
            dve.wait_ge(s_tab, 7)
            dve.tensor_reduce(jumps[:, :], jumped[:, :, :], AX.X, ALU.add).then_inc(s_tab, 1)
            dve.wait_ge(s_tab, 8)
            dve.scalar_tensor_tensor(out=tile_base[:, :], in0=tile_no[:, :], scalar=float(S), in1=jumps[:, :],
                                     op0=ALU.mult, op1=ALU.add).then_inc(s_tab, 1)
            dve.wait_ge(s_tab, 9)
            dve.tensor_copy(base_int[:, :], tile_base[:, :]).then_inc(s_base, 1)
            dve.tensor_reduce(tile_expert[:, :], passed[:, :, 0:E - 1], AX.X, ALU.add).then_inc(s_tab, 1)
            dve.wait_ge(s_tab, 10)
            dve.tensor_copy(expert_int[:, :], tile_expert[:, :]).then_inc(s_expert, 1)

            dve.tensor_tensor(gate_exp[:, :, :], sorted_logits[:, :, :],
                              sorted_logits[:, :, 0:1].to_broadcast([P, TILES, E]), ALU.subtract).then_inc(s_gate, 1)
            dve.wait_ge(s_gexp, 1)
            dve.tensor_reduce(gate_sum[:, :], gate_exp[:, :, :], AX.X, ALU.add)
            dve.tensor_tensor(gate_den[:, 0, :], gate_exp[:, :, 0], gate_exp[:, :, 1], ALU.add).then_inc(s_gate, 1)
            dve.wait_ge(s_gate, 2)
            dve.scalar_tensor_tensor(out=gate_den[:, 1, :], in0=gate_sum[:, :], scalar=GATE_EPS, in1=gate_den[:, 0, :],
                                     op0=ALU.mult, op1=ALU.add).then_inc(s_gate, 1)
            dve.wait_ge(s_gate, 3)
            dve.reciprocal(gate_inv[:, :], gate_den[:, 1, :]).then_inc(s_gate, 1)
            dve.wait_ge(s_gate, 4)
            for c in range(TOP):
                ins = dve.tensor_tensor(gates[:, c, :], gate_exp[:, :, c], gate_inv[:, :], ALU.mult)
            ins.then_inc(s_gate, 1)
            dve.wait_ge(s_gate, 5)

            def weights_low(i, expert):
                r = i.ring(2)
                dve.wait_ge(s_uphi, i.plus(1).n)
                dve.tensor_tensor(up_lo[:, r, :], ew13_sb[:, bass.ds(expert * (2 * EHP), 2 * EHP)],
                                  up_hi[:, r, :].bitcast(F32), ALU.subtract)

            def rows_low(i):
                r = i.ring(2)
                dve.wait_ge(s_xhi, i.plus(1).n)
                dve.tensor_tensor(rows_lo[:, r, :], slots_ps, rows_hi[:, r, :].bitcast(F32),
                                  ALU.subtract).then_inc(s_xlo, 1)

            def product(i):
                r = i.ring(2)
                dve.wait_ge(s_silu1, i.plus(1).n)
                dve.wait_ge(s_h3, i.plus(1).n)
                dve.tensor_tensor(prod[:, r, :], h3_ps[r], silu1[:, r, :], ALU.mult).then_inc(s_prod, 1)

            def keep_result(i):
                dve.wait_ge(s_yy, i.plus(1).n)
                if positive(i.turn(4)):
                    dve.wait_ge(s_resout[i.ring(4)], i.turn(4) * (16 * ST))
                dve.tensor_copy(result[:, i.ring(4), :, :].rearrange("p h d -> p (h d)"),
                                result_ps).then_inc(s_res, 1)

            def expert_step(i, next_expert):
                if i.plus(-2).within(SLOT_TILES):
                    keep_result(i.plus(-2))
                if i.plus(1).within(SLOT_TILES):
                    weights_low(i.plus(1), next_expert)
                    rows_low(i.plus(1))
                if i.within(SLOT_TILES):
                    product(i)

            run_expert_steps(dve, mybir.EngineType.DVE, 1, expert_step)

            def add_second(g):
                r = g.ring(4)
                dve.wait_ge(s_picked[r], g.turn(4) * 32 + 32)
                for t in range(FG):
                    mine = tokens[:, g.n * FG + t, :]
                    ins = dve.scalar_tensor_tensor(
                        out=mine, in0=picked[:, r, 1, t, :], scalar=gates[:, 1, bass.ds(g.n * FG + t, 1)],
                        in1=mine, op0=ALU.mult, op1=ALU.add)
                ins.then_inc(s_second, 1)

            def add_first(g):
                dve.wait_ge(s_second, g.plus(1).n)
                dve.wait_ge(s_first, g.plus(1).n)
                mine = tokens[:, bass.ds(g.n * FG, FG), :]
                dve.tensor_tensor(mine, picked[:, g.ring(4), 0, :, :], mine, ALU.add).then_inc(s_sum, 1)

            STEPS = TILES // FG
            add_second(Step(0, 0))
            with dve.Fori(0, STEPS // UNROLL - 1) as k:
                for q in range(UNROLL):
                    add_second(Step(k, q + 1))
                    add_first(Step(k, q))
            for q in range(STEPS - UNROLL, STEPS):
                if q + 1 < STEPS:
                    add_second(Step(0, q + 1))
                add_first(Step(0, q))


def kernel(x, adj, L0_gnn_epsilon, L0_gnn_W1, L0_gnn_b1, L0_gnn_rms_weight, L0_gnn_W2, L0_gnn_b2,
           L0_ffn_router_w, L0_ffn_w1, L0_ffn_w2, L0_ffn_w3):
    import numpy as np
    from concourse import bacc
    from concourse.bass_utils import run_bass_kernel_spmd

    def up_weights(w):
        padded = np.zeros((D, E, EHP), w.dtype)
        padded[:, :, :EH] = np.transpose(w, (2, 0, 1))
        return padded

    def down_weights(w):
        padded = np.zeros((E, EHP, D), w.dtype)
        padded[:, :EH] = np.transpose(w, (0, 2, 1))
        return np.transpose(padded.reshape(E, CHUNKS, HK, D), (2, 0, 1, 3)).reshape(HK, E * CHUNKS * D)

    a = {k: np.asarray(v) for k, v in dict(
        x=x, adj=adj, eps=L0_gnn_epsilon, w1=L0_gnn_W1, b1=L0_gnn_b1, rms_w=L0_gnn_rms_weight, w2=L0_gnn_W2,
        b2=L0_gnn_b2, router=L0_ffn_router_w, ew1=L0_ffn_w1, ew2=L0_ffn_w2, ew3=L0_ffn_w3).items()}
    arrays = dict(
        x=a["x"].reshape(TOKENS, D),
        adj_t=np.transpose(a["adj"], (0, 2, 1)).reshape(TOKENS, N),
        eps=np.broadcast_to(a["eps"].reshape(1, 1), (P, 1)),
        w1=a["w1"],
        biases=np.concatenate([a["b1"], a["b2"]]).reshape(P, BIAS // P),
        rms_w=np.broadcast_to(a["rms_w"][None], (P, H)),
        w2=a["w2"],
        router_t=a["router"].T,
        ew13=np.stack([up_weights(a["ew1"]), up_weights(a["ew3"])], axis=2).reshape(D, E * 2 * EHP),
        ew2=down_weights(a["ew2"]),
    )
    arrays = {f"in_{k}": np.ascontiguousarray(v) for k, v in arrays.items()}
    nc = bacc.Bacc("TRN2", target_bir_lowering=False, num_devices=1)
    ap = {k[3:]: nc.dram_tensor(k, v.shape, F32, kind="ExternalInput").ap() for k, v in arrays.items()}
    out = nc.dram_tensor("out", (TOKENS, D), F32, kind="ExternalOutput").ap()
    graph_moe_kernel(nc, ap["x"], ap["adj_t"], ap["eps"], ap["w1"], ap["biases"], ap["rms_w"], ap["w2"],
                     ap["router_t"], ap["ew13"], ap["ew2"], out)
    r = run_bass_kernel_spmd(nc, [arrays], core_ids=[0])
    return r.results[0]["out"].reshape(GRAPHS, N, D)
```
